# Optimizing a Trainium2 kernel written in Bass

```python
import numpy as np
import jax
import jax.numpy as jnp

def _softmax(x, axis=-1):
    return jax.nn.softmax(x, axis=axis)

def _gelu(x):
    return jax.nn.gelu(x, approximate=True)

def _silu(x):
    return jax.nn.silu(x)

def _sigmoid(x):
    return jax.nn.sigmoid(x)

def _layernorm(x, axis=-1, eps=1e-05):
    m = jnp.mean(x, axis=axis, keepdims=True)
    v = jnp.var(x, axis=axis, keepdims=True)
    return (x - m) / jnp.sqrt(v + eps)

def _scatter_add(tgt, idx, src, axis=0):
    return tgt.at[idx].add(src)

def _segment_sum(src, seg, n):
    return jax.ops.segment_sum(src, seg, n)
kernel_name = 'mk_prb_d1_jaxref_r8_a0e742'

def setup_inputs(seed: int=0):
    np.random.seed(seed)
    _w = jnp.asarray

    def _L0_attn_setup():
        import math
        import jax, jax.numpy as jnp
        import numpy as np
        D, DK, DV = (128, 128, 128)
        B, S = (4, 256)
        key = jax.random.key(seed)
        ks = jax.random.split(key, 4)
        std_qk = math.sqrt(2.0 / (D + DK))
        std_v = math.sqrt(2.0 / (D + DV))
        return {'X': jax.random.normal(ks[0], (B, S, D), dtype=jnp.float32), 'W_q': jax.random.normal(ks[1], (D, DK), dtype=jnp.float32) * std_qk, 'W_k': jax.random.normal(ks[2], (D, DK), dtype=jnp.float32) * std_qk, 'W_v': jax.random.normal(ks[3], (D, DV), dtype=jnp.float32) * std_v, 'b_q': jnp.zeros((DK,), dtype=jnp.float32), 'b_k': jnp.zeros((DK,), dtype=jnp.float32), 'b_v': jnp.zeros((DV,), dtype=jnp.float32)}
    _L0_attn_in = _L0_attn_setup()

    def _L0_ffn_setup():
        import jax, jax.numpy as jnp
        import numpy as np
        DIM = 128
        DEPTH = 6
        HEADS = 16
        DIM_HEAD = 64
        WINDOW = 32
        INNER = HEADS * DIM_HEAD
        DIM_INNER = int(DIM * 4 * 2 / 3)
        QK_SCALE = 8.0

        def shift_tokens(t):
            a, s = jnp.split(t, 2, -1)
            s = jnp.pad(s, ((0, 0), (1, 0), (0, 0)))[:, :-1]
            return jnp.concatenate([a, s], -1)

        def l2norm(t):
            return t / jnp.maximum(jnp.linalg.norm(t, axis=-1, keepdims=True), 1e-12)

        def rotate_half(x):
            x1, x2 = jnp.split(x, 2, -1)
            return jnp.concatenate([-x2, x1], -1)

        def rotary_tables(n):
            half = jnp.arange(0, DIM_HEAD, 2, dtype=jnp.float32)
            inv_freq = 1.0 / 10000.0 ** (half / DIM_HEAD)
            t = jnp.arange(n, dtype=jnp.float32)
            freqs = t[:, None] * inv_freq[None, :]
            freqs = jnp.concatenate([freqs, freqs], -1)
            base_scale = (half + 0.4 * DIM_HEAD) / (1.4 * DIM_HEAD)
            power = (t - n // 2) / (WINDOW // 2)
            scale = base_scale[None, :] ** power[:, None]
            scale = jnp.concatenate([scale, scale], -1)
            return (freqs, scale)

        def local_attention(q, k, v):
            b, h, n, d = q.shape
            w = WINDOW
            nw = n // w
            bq = q.reshape(b, h, nw, w, d)
            bk = k.reshape(b, h, nw, w, d)
            bv = v.reshape(b, h, nw, w, d)

            def look(t):
                p = jnp.pad(t, ((0, 0), (0, 0), (1, 0), (0, 0), (0, 0)))
                return jnp.concatenate([p[:, :, :nw], p[:, :, 1:]], axis=3)
            bk2, bv2 = (look(bk), look(bv))
            seq = jnp.arange(n).reshape(nw, w)
            seq_p = jnp.pad(seq, ((1, 0), (0, 0)), constant_values=-1)
            jt = jnp.concatenate([seq_p[:nw], seq_p[1:]], axis=1)
            it = seq[:, :, None]
            jb = jt[:, None, :]
            mask = (it < jb) | (it > jb + w) | (jb == -1)
            sim = jnp.einsum('bhwie,bhwje->bhwij', bq, bk2) * QK_SCALE
            sim = jnp.where(mask, -jnp.finfo(sim.dtype).max, sim)
            attn = jax.nn.softmax(sim, -1)
            out = jnp.einsum('bhwij,bhwje->bhwie', attn, bv2)
            return out.reshape(b, h, n, d)

        def attn_layer(x, Wqkv, qs, ksc, Wo):
            b, n, _ = x.shape
            qkv = x @ Wqkv
            q, k, v = jnp.split(qkv, 3, -1)
            sh = lambda t: t.reshape(b, n, HEADS, DIM_HEAD).transpose(0, 2, 1, 3)
            q, k, v = (sh(q), sh(k), sh(v))
            q = l2norm(q) * qs
            k = l2norm(k) * ksc
            freqs, scale = rotary_tables(n)
            cos, sin = (jnp.cos(freqs), jnp.sin(freqs))
            q = q * cos * scale + rotate_half(q) * sin * scale
            inv = 1.0 / scale
            k = k * cos * inv + rotate_half(k) * sin * inv
            out = local_attention(q, k, v)
            out = out.transpose(0, 2, 1, 3).reshape(b, n, INNER)
            return out @ Wo

        def ffn_layer(x, g, bln, W1, b1, W2, b2):
            mu = x.mean(-1, keepdims=True)
            var = ((x - mu) ** 2).mean(-1, keepdims=True)
            xn = (x - mu) / jnp.sqrt(var + 1e-05) * g + bln
            hg = xn @ W1 + b1
            a, gate = jnp.split(hg, 2, -1)
            return a * jax.nn.gelu(gate, approximate=False) @ W2 + b2
        key = jax.random.key(seed)
        ks = jax.random.split(key, 8)
        B, N = (2, 256)
        init = lambda k, shape: jax.random.normal(k, shape, jnp.float32) * 0.02
        return {'x': jax.random.normal(ks[0], (B, N, DIM), jnp.float32), 'Wqkv': init(ks[1], (DEPTH, DIM, 3 * INNER)), 'q_scale': jnp.ones((DEPTH, DIM_HEAD), jnp.float32), 'k_scale': jnp.ones((DEPTH, DIM_HEAD), jnp.float32), 'Wo': init(ks[2], (DEPTH, INNER, DIM)), 'ln_g': jnp.ones((DEPTH, DIM), jnp.float32), 'ln_b': jnp.zeros((DEPTH, DIM), jnp.float32), 'W1': init(ks[3], (DEPTH, DIM, 2 * DIM_INNER)), 'b1': jnp.zeros((DEPTH, 2 * DIM_INNER), jnp.float32), 'W2': init(ks[4], (DEPTH, DIM_INNER, DIM)), 'b2': jnp.zeros((DEPTH, DIM), jnp.float32)}
    _L0_ffn_in = _L0_ffn_setup()
    _d = {'L0_attn_X': _L0_attn_in['X'], 'L0_attn_W_q': _L0_attn_in['W_q'], 'L0_attn_W_k': _L0_attn_in['W_k'], 'L0_attn_W_v': _L0_attn_in['W_v'], 'L0_attn_b_q': _L0_attn_in['b_q'], 'L0_attn_b_k': _L0_attn_in['b_k'], 'L0_attn_b_v': _L0_attn_in['b_v'], 'L0_ffn_Wqkv': _L0_ffn_in['Wqkv'], 'L0_ffn_q_scale': _L0_ffn_in['q_scale'], 'L0_ffn_k_scale': _L0_ffn_in['k_scale'], 'L0_ffn_Wo': _L0_ffn_in['Wo'], 'L0_ffn_ln_g': _L0_ffn_in['ln_g'], 'L0_ffn_ln_b': _L0_ffn_in['ln_b'], 'L0_ffn_W1': _L0_ffn_in['W1'], 'L0_ffn_b1': _L0_ffn_in['b1'], 'L0_ffn_W2': _L0_ffn_in['W2'], 'L0_ffn_b2': _L0_ffn_in['b2']}
    _x0 = _d['L0_attn_X']
    _d['L0_attn_X'] = jax.random.normal(jax.random.fold_in(jax.random.key(seed), 1), (8, 256, 128), dtype=_x0.dtype)
    del _x0
    return _d

def reference(L0_attn_X, L0_attn_W_q, L0_attn_W_k, L0_attn_W_v, L0_attn_b_q, L0_attn_b_k, L0_attn_b_v, L0_ffn_Wqkv, L0_ffn_q_scale, L0_ffn_k_scale, L0_ffn_Wo, L0_ffn_ln_g, L0_ffn_ln_b, L0_ffn_W1, L0_ffn_b1, L0_ffn_W2, L0_ffn_b2):

    def _L0_attn_ref(X, W_q, W_k, W_v, b_q, b_k, b_v):
        import math
        import jax, jax.numpy as jnp
        import numpy as np
        D, DK, DV = (128, 128, 128)
        B, S = (4, 256)
        scale = 1.0 / math.sqrt(DK)
        Q = X @ W_q + b_q
        K = X @ W_k + b_k
        V = X @ W_v + b_v
        A = jnp.einsum('bsd,btd->bst', Q, K) * scale
        A = jax.nn.softmax(A, axis=2)
        return jnp.einsum('bst,btv->bsv', A, V)

    def _L0_ffn_ref(x, Wqkv, q_scale, k_scale, Wo, ln_g, ln_b, W1, b1, W2, b2):
        import jax, jax.numpy as jnp
        import numpy as np
        DIM = 128
        DEPTH = 6
        HEADS = 16
        DIM_HEAD = 64
        WINDOW = 32
        INNER = HEADS * DIM_HEAD
        DIM_INNER = int(DIM * 4 * 2 / 3)
        QK_SCALE = 8.0

        def shift_tokens(t):
            a, s = jnp.split(t, 2, -1)
            s = jnp.pad(s, ((0, 0), (1, 0), (0, 0)))[:, :-1]
            return jnp.concatenate([a, s], -1)

        def l2norm(t):
            return t / jnp.maximum(jnp.linalg.norm(t, axis=-1, keepdims=True), 1e-12)

        def rotate_half(x):
            x1, x2 = jnp.split(x, 2, -1)
            return jnp.concatenate([-x2, x1], -1)

        def rotary_tables(n):
            half = jnp.arange(0, DIM_HEAD, 2, dtype=jnp.float32)
            inv_freq = 1.0 / 10000.0 ** (half / DIM_HEAD)
            t = jnp.arange(n, dtype=jnp.float32)
            freqs = t[:, None] * inv_freq[None, :]
            freqs = jnp.concatenate([freqs, freqs], -1)
            base_scale = (half + 0.4 * DIM_HEAD) / (1.4 * DIM_HEAD)
            power = (t - n // 2) / (WINDOW // 2)
            scale = base_scale[None, :] ** power[:, None]
            scale = jnp.concatenate([scale, scale], -1)
            return (freqs, scale)

        def local_attention(q, k, v):
            b, h, n, d = q.shape
            w = WINDOW
            nw = n // w
            bq = q.reshape(b, h, nw, w, d)
            bk = k.reshape(b, h, nw, w, d)
            bv = v.reshape(b, h, nw, w, d)

            def look(t):
                p = jnp.pad(t, ((0, 0), (0, 0), (1, 0), (0, 0), (0, 0)))
                return jnp.concatenate([p[:, :, :nw], p[:, :, 1:]], axis=3)
            bk2, bv2 = (look(bk), look(bv))
            seq = jnp.arange(n).reshape(nw, w)
            seq_p = jnp.pad(seq, ((1, 0), (0, 0)), constant_values=-1)
            jt = jnp.concatenate([seq_p[:nw], seq_p[1:]], axis=1)
            it = seq[:, :, None]
            jb = jt[:, None, :]
            mask = (it < jb) | (it > jb + w) | (jb == -1)
            sim = jnp.einsum('bhwie,bhwje->bhwij', bq, bk2) * QK_SCALE
            sim = jnp.where(mask, -jnp.finfo(sim.dtype).max, sim)
            attn = jax.nn.softmax(sim, -1)
            out = jnp.einsum('bhwij,bhwje->bhwie', attn, bv2)
            return out.reshape(b, h, n, d)

        def attn_layer(x, Wqkv, qs, ksc, Wo):
            b, n, _ = x.shape
            qkv = x @ Wqkv
            q, k, v = jnp.split(qkv, 3, -1)
            sh = lambda t: t.reshape(b, n, HEADS, DIM_HEAD).transpose(0, 2, 1, 3)
            q, k, v = (sh(q), sh(k), sh(v))
            q = l2norm(q) * qs
            k = l2norm(k) * ksc
            freqs, scale = rotary_tables(n)
            cos, sin = (jnp.cos(freqs), jnp.sin(freqs))
            q = q * cos * scale + rotate_half(q) * sin * scale
            inv = 1.0 / scale
            k = k * cos * inv + rotate_half(k) * sin * inv
            out = local_attention(q, k, v)
            out = out.transpose(0, 2, 1, 3).reshape(b, n, INNER)
            return out @ Wo

        def ffn_layer(x, g, bln, W1, b1, W2, b2):
            mu = x.mean(-1, keepdims=True)
            var = ((x - mu) ** 2).mean(-1, keepdims=True)
            xn = (x - mu) / jnp.sqrt(var + 1e-05) * g + bln
            hg = xn @ W1 + b1
            a, gate = jnp.split(hg, 2, -1)
            return a * jax.nn.gelu(gate, approximate=False) @ W2 + b2
        for i in range(DEPTH):
            x = attn_layer(shift_tokens(x), Wqkv[i], q_scale[i], k_scale[i], Wo[i]) + x
            x = ffn_layer(shift_tokens(x), ln_g[i], ln_b[i], W1[i], b1[i], W2[i], b2[i]) + x
        return x
    x = L0_attn_X
    xn = _layernorm(x, axis=-1)
    x = x + _L0_attn_ref(xn, L0_attn_W_q, L0_attn_W_k, L0_attn_W_v, L0_attn_b_q, L0_attn_b_k, L0_attn_b_v) + _L0_ffn_ref(xn, L0_ffn_Wqkv, L0_ffn_q_scale, L0_ffn_k_scale, L0_ffn_Wo, L0_ffn_ln_g, L0_ffn_ln_b, L0_ffn_W1, L0_ffn_b1, L0_ffn_W2, L0_ffn_b2)
    return x

_drawn_inputs = setup_inputs


def setup_inputs(seed=0):
    import zlib

    import numpy as np

    out = dict(_drawn_inputs(seed))
    spreads = {'L0_attn_b_q': (0.0, 2.0),
     'L0_attn_b_k': (0.0, 2.0),
     'L0_attn_b_v': (0.0, 0.456),
     'L0_ffn_q_scale': (1.0, 0.6),
     'L0_ffn_k_scale': (1.0, 0.6),
     'L0_ffn_ln_g': (1.0, 0.6),
     'L0_ffn_ln_b': (0.0, 0.8),
     'L0_ffn_b1': (0.0, 0.8),
     'L0_ffn_b2': (0.0, 0.1)}
    factors = {'L0_ffn_W1': 3.654, 'L0_ffn_W2': 3.586, 'L0_attn_W_q': 2.682}
    for name, (base, spread) in spreads.items():
        noise = np.random.default_rng([zlib.crc32(name.encode()), seed]).standard_normal(out[name].shape)
        drawn = base * np.exp(spread * noise) if base else spread * noise
        out[name] = jnp.asarray(drawn.astype(out[name].dtype))
    for name, factor in factors.items():
        out[name] = (out[name] * factor).astype(out[name].dtype)
    return out
```

```python
from contextlib import ExitStack

import concourse.bass as bass
import numpy as np
from concourse import mybir

F32 = mybir.dt.float32
BF16 = mybir.dt.bfloat16
ALU = mybir.AluOpType
ACT = mybir.ActivationFunctionType
AX = mybir.AxisListType

P = 128
SEQS, LEN = 8, 256
TILES = LEN // P
DEPTH, HEADS, DH, WIN = 6, 16, 64, 32
INNER = HEADS * DH
PAIRS = HEADS // 2
HID = int(P * 4 * 2 / 3)
HCH = 3
HLAST = HID - 2 * P
STEPS = DEPTH * SEQS
CH = 512
CHH = CH // DH
QKV = 3 * INNER
UNITS = 4
WLOADS = 8
MASKED = -1.0e30
EPS = 1e-5


def nth(per, n, e):
    value = n * per + e
    if isinstance(value, int):
        return max(0, value)
    assert value.min_val > 0
    return value


def live(n):
    return not isinstance(n, int) or 0 <= n < STEPS


def program(nc, X, Wq, Wk, Wv, bq, bk, bv, Wqkv, q_scale, k_scale, Wo, ln_g, ln_b, W1, b1, W2, b2,
            rot_base, masks, ident_f, out):
    ctx = ExitStack()
    with ctx:
        def sb(name, cols, dt=F32):
            return ctx.enter_context(nc.sbuf_tensor(name, [P, cols], dt))

        def sem(name):
            return ctx.enter_context(nc.semaphore(name))

        ident = sb("ident", P)
        identh = sb("identh", P, BF16)
        mask = sb("mask", 2 * 64, BF16)
        maskf = sb("maskf", 2 * 64)
        x_tok = sb("x_tok", SEQS * TILES * P)
        acc = sb("acc", SEQS * TILES * P)
        w_qkv = sb("w_qkv", 2 * QKV)
        w_o = sb("w_o", 2 * PAIRS * P)
        w_1 = sb("w_1", 2 * 2 * HID)
        w_2 = sb("w_2", 2 * HCH * P)
        b_1 = sb("b_1", 2 * 2 * HID)
        gain = sb("gain", DEPTH)
        shift = sb("shift", DEPTH)
        rbase = sb("rbase", 4 * TILES * DH)
        scales = sb("scales", 2 * DEPTH * DH)
        rtab = sb("rtab", DEPTH * 4 * TILES * DH)
        xin = sb("xin", TILES * P)
        xs = sb("xs", LEN)
        sq = sb("sq", 2 * CH)
        t1 = sb("t1", 2 * CH)
        t2 = sb("t2", 2 * CH)
        rot = sb("rot", TILES * 4 * CH)
        n2 = sb("n2", TILES * 2 * HEADS)
        n2c = sb("n2c", TILES * 2 * HEADS)
        rnorm = sb("rnorm", TILES * 2 * HEADS)
        minus_half = sb("minus_half", 2 * HEADS)
        eps = sb("eps", TILES)
        qz = sb("qz", PAIRS * 8 * 64)
        kt = sb("kt", PAIRS * (WIN + LEN))
        v = sb("v", TILES * INNER)
        vb = sb("vb", TILES * INNER)
        es = sb("es", 2 * CH)
        m8 = sb("m8", 2 * PAIRS)
        s8 = sb("s8", 2 * PAIRS)
        r8 = sb("r8", 2 * PAIRS)
        pz = sb("pz", 2 * PAIRS * P)
        ot = sb("ot", PAIRS * LEN)
        xm = sb("xm", TILES * P)
        xf = sb("xf", LEN)
        stat = sb("stat", TILES * 6)
        mv = sb("mv", TILES * 2)
        ve = sb("ve", TILES)
        rstd = sb("rstd", TILES)
        xn = sb("xn", TILES * P)
        xg = sb("xg", LEN)
        gt = sb("gt", HID)
        gg = sb("gg", HID)
        am = sb("am", HID)
        hm = sb("hm", HID)
        ht = sb("ht", HCH * P)
        aw = sb("aw", 3 * P)
        abq = sb("abq", 2)
        abv = sb("abv", P)
        st0 = sb("st0", SEQS * TILES * 6)
        mv0 = sb("mv0", SEQS * TILES * 2)
        ve0 = sb("ve0", SEQS * TILES)
        rs0 = sb("rs0", SEQS * TILES)
        axin = sb("axin", LEN)
        ax = sb("ax", LEN)
        aq = sb("aq", LEN)
        ak = sb("ak", LEN)
        av = sb("av", LEN)
        am2 = sb("am2", TILES)
        ap_ = sb("ap_", TILES * LEN)
        as2 = sb("as2", TILES)
        ar2 = sb("ar2", TILES)
        apt = sb("apt", TILES * LEN)

        bank = [ctx.enter_context(nc.psum_tensor(f"bank{i}", [P, CH], F32)) for i in range(8)]
        pQ = bank[0:2]
        pT, pS, pP, pO, pF, pG = bank[2:8]

        s_const = sem("s_const")
        s_x = sem("s_x")
        s_w = sem("s_w")
        s_zero = sem("s_zero")
        s_rbase = sem("s_rbase")
        s_xready = sem("s_xready")
        s_xin = sem("s_xin")
        s_xt = sem("s_xt")
        s_xs = sem("s_xs")
        s_qkv = sem("s_qkv")
        s_sq = sem("s_sq")
        s_t1 = sem("s_t1")
        s_rot = sem("s_rot")
        s_n2 = sem("s_n2")
        s_add = sem("s_add")
        s_n2c = sem("s_n2c")
        s_rn = sem("s_rn")
        s_qsc = sem("s_qsc")
        s_ksc = sem("s_ksc")
        s_qt = sem("s_qt")
        s_qte = sem("s_qte")
        s_v = sem("s_v")
        s_vb0 = sem("s_vb0")
        s_vb1 = sem("s_vb1")
        s_s = sem("s_s")
        s_max = sem("s_max")
        s_sub = sem("s_sub")
        s_exp = sem("s_exp")
        s_sum = sem("s_sum")
        s_rec = sem("s_rec")
        s_p = sem("s_p")
        s_pt = sem("s_pt")
        s_pte = sem("s_pte")
        s_av = sem("s_av")
        s_ot = sem("s_ot")
        s_wo = sem("s_wo")
        s_mid = sem("s_mid")
        s_res = sem("s_res")
        s_f1 = sem("s_f1")
        s_xf = sem("s_xf")
        s_f2 = sem("s_f2")
        s_st = sem("s_st")
        s_mv = sem("s_mv")
        s_ve = sem("s_ve")
        s_rstd = sem("s_rstd")
        s_xn = sem("s_xn")
        s_f3 = sem("s_f3")
        s_xg = sem("s_xg")
        s_f4 = sem("s_f4")
        s_gt = sem("s_gt")
        s_gg = sem("s_gg")
        s_am = sem("s_am")
        s_hm = sem("s_hm")
        s_f5 = sem("s_f5")
        s_ht = sem("s_ht")
        s_f6 = sem("s_f6")
        s_fin0 = sem("s_fin0")
        s_l0 = sem("s_l0")
        s_l0p = sem("s_l0p")
        s_a = {k: sem("s_a_" + k) for k in ("xin", "t", "x", "qkv", "q", "k", "v", "s", "max", "neg", "exp",
                                            "rec", "pt", "pte", "o", "done")}
        s_fin = sem("s_fin")
        s_out = sem("s_out")

        def layer(n):
            return n // SEQS

        def par(n):
            return (n // SEQS) % 2

        def tokens(t, n, T, k=1):
            return t[:, bass.ds((n % SEQS) * (TILES * P) + T * P, k * P)]

        def heads(a):
            return a.rearrange("p (h c) -> p h c", c=DH)

        def table(n, kind, T, half=None):
            off = layer(n) * (4 * TILES * DH) + (kind * TILES + T) * DH
            w = DH
            if half is not None:
                off, w = off + half * (DH // 2), DH // 2
            return rtab[:, bass.ds(off, w)].unsqueeze(1).to_broadcast([P, CHH, w])

        def over(a, k, w):
            return a.unsqueeze(2).to_broadcast([P, k, w])

        qz5 = qz[:, :].rearrange("p (a w h q) -> p a w h q", a=PAIRS, w=8, h=2)
        kt3 = kt[:, :].rearrange("p (a t) -> p a t", a=PAIRS)
        pz4 = pz[:, :].rearrange("p (b a s c) -> p b a s c", b=2, a=PAIRS, s=2)
        pz5 = pz[:, :].rearrange("p (b a s h q) -> p b a s h q", b=2, a=PAIRS, s=2, h=2)
        ot6 = ot[:, :].rearrange("p (a t s l q) -> p a t s l q", a=PAIRS, t=TILES, s=2, l=2)

        block = ctx.enter_context(nc.Block())

        def chunk_of(i):
            return i * CH, (i if i < 4 else None)

        @block.sync
        def _(sp):
            sp.dma_start(acc[:, :].rearrange("p (s t c) -> p s t c", s=SEQS, t=TILES),
                         X.rearrange("s (t p) c -> p s t c", p=P)).then_inc(s_x, 16)
            for dst, src in ((ident[:, :], ident_f), (maskf[:, :], masks),
                             (rbase[:, :], rot_base),
                             (aw[:, 0:P], Wq), (aw[:, P:2 * P], Wk), (aw[:, 2 * P:3 * P], Wv),
                             (abq[:, 0:1], bq.rearrange("(p a) -> p a", a=1)),
                             (abq[:, 1:2], bk.rearrange("(p a) -> p a", a=1)),
                             (abv[:, :], bv.partition_broadcast(P)),
                             (scales[:, 0:DEPTH * DH], q_scale.rearrange("l c -> (l c)").partition_broadcast(P)),
                             (scales[:, DEPTH * DH:], k_scale.rearrange("l c -> (l c)").partition_broadcast(P)),
                             ):
                sp.dma_start(dst, src).then_inc(s_const, 16)
            for dst, src in ((gain, ln_g), (shift, ln_b)):
                sp.dma_start(dst[:, :], src.rearrange("l c -> c l"), allow_slow_non_contiguous=True)\
                  .then_inc(s_const, 16)

            def weights(l):
                p = l % 2
                sp.dma_start(w_qkv[:, bass.ds(p * QKV, QKV)], Wqkv[bass.ds(l * P, P), :]).then_inc(s_w, 16)
                sp.dma_start(w_o[:, bass.ds(p * PAIRS * P, PAIRS * P)].rearrange("p (a c) -> p a c", a=PAIRS),
                             Wo[bass.ds(l * INNER, INNER), :].rearrange("(a p) c -> p a c", p=P)).then_inc(s_w, 16)
                sp.dma_start(w_1[:, bass.ds(p * 2 * HID, 2 * HID)], W1[bass.ds(l * P, P), :]).then_inc(s_w, 16)
                for j in range(HCH):
                    rows = P if j < 2 else HLAST
                    sp.dma_start(w_2[0:rows, bass.ds(p * HCH * P + j * P, P)],
                                 W2[bass.ds(l * HID + j * P, rows), :]).then_inc(s_w, 16)
                sp.dma_start(w_2[HLAST:HLAST + 1, bass.ds(p * HCH * P + 2 * P, P)], b2[bass.ds(l, 1), :])\
                  .then_inc(s_w, 16)
                sp.dma_start(b_1[:, bass.ds(p * 2 * HID, 2 * HID)],
                             b1[bass.ds(l, 1), :].to_broadcast([P, 2 * HID])).then_inc(s_w, 16)

            weights(0)
            weights(1)

            def copy_v(n):
                sp.wait_ge(s_v, nth(4, n, 2))
                sp.dma_start(vb[WIN:P, 0:INNER], v[0:P - WIN, 0:INNER]).then_inc(s_vb0, 16)
                sp.wait_ge(s_av, nth(4, n - 1, 3))
                sp.dma_start(vb[0:WIN, INNER:], v[P - WIN:P, 0:INNER]).then_inc(s_vb0, 16)
                sp.wait_ge(s_v, nth(4, n, 4))
                sp.dma_start(vb[WIN:P, INNER:], v[0:P - WIN, INNER:]).then_inc(s_vb1, 16)

            sp.wait_ge(s_zero, 2)
            copy_v(0)
            with sp.Fori(1, SEQS) as n:
                copy_v(n)
            with sp.Fori(1, DEPTH - 1) as l:
                copy_v(l * SEQS)
                copy_v(l * SEQS + 1)
                done = sp.snap(l * SEQS + SEQS)
                sp.wait_ge(s_zero, 2)
                sp.wait_ge(s_xready, done)
                weights(l + 1)
                with sp.Fori(2, SEQS) as k:
                    copy_v(l * SEQS + k)
            with sp.Fori((DEPTH - 1) * SEQS, STEPS) as n:
                copy_v(n)
            sp.wait_ge(s_fin, 1)
            sp.dma_start(out.rearrange("s (t p) c -> p s t c", p=P),
                         acc[:, :].rearrange("p (s t c) -> p s t c", s=SEQS, t=TILES)).then_inc(s_out, 16)
            sp.wait_ge(s_out, 16)

        NCONST = 13

        @block.gpsimd
        def _(pool):
            g = nc.gpsimd
            g.memset(minus_half[:, :], -0.5)
            g.memset(eps[:, :], EPS)
            g.memset(qz[:, :], 0.0)
            g.memset(kt[:, :], 0.0)
            g.memset(xs[:, :], 0.0)
            g.memset(xf[:, :], 0.0).then_inc(s_zero, 1)
            pool.wait_ge(s_l0, 2 * SEQS * TILES)
            g.tensor_scalar(ve0[:, :].unsqueeze(2), mv0[:, :].rearrange("p (k a) -> p k a", a=2)[:, :, 1:2],
                            EPS, 1.0, ALU.add, ALU.mult).then_inc(s_l0p, 1)
            pool.wait_ge(s_l0p, 1)
            g.tensor_tensor(rs0[:, :], ve0[:, :], minus_half[:, 0:SEQS * TILES], ALU.pow).then_inc(s_l0p, 1)

            def copy_in(n):
                pool.wait_ge(s_xready, nth(1, n, 1))
                pool.wait_ge(s_xt, nth(1, n - 1, 1))
                g.tensor_copy(xin[:, :], tokens(x_tok, n, 0, TILES)).then_inc(s_xin, 1)

            def add(n, T, m):
                i = 4 * T + m
                pool.wait_ge(s_rot, nth(8, n, i + 1))
                pool.wait_ge(s_qt, nth(8, n - 1, 4 * T + 4))
                b = (m % 2) * CH
                g.tensor_tensor(rot[:, i * CH:(i + 1) * CH], t1[:, b:b + CH], t2[:, b:b + CH], ALU.add)\
                 .then_inc(s_add, 1)

            def norms(n, T):
                w = slice(T * 2 * HEADS, (T + 1) * 2 * HEADS)
                pool.wait_ge(s_n2c, nth(2, n, T + 1))
                pool.wait_ge(s_ksc, nth(4, n - 1, 2 * T + 2))
                g.tensor_tensor(rnorm[:, w], n2c[:, w], minus_half[:, :], ALU.pow).then_inc(s_rn, 1)
                pool.wait_ge(s_rn, nth(2, n, T + 1))

            def scale_q(n, T, m):
                pool.wait_ge(s_add, nth(8, n, 4 * T + m + 1))
                c = heads(rot[:, (4 * T + m) * CH:(4 * T + m + 1) * CH])
                r = rnorm[:, T * 2 * HEADS + m * CHH:T * 2 * HEADS + (m + 1) * CHH]
                g.tensor_tensor(c, c, over(r, CHH, DH), ALU.mult).then_inc(s_qsc, 1)

            def residual(n):
                pool.wait_ge(s_mid, nth(2, n, 2))
                g.tensor_copy(tokens(x_tok, n, 0, TILES), xm[:, :]).then_inc(s_res, 1)

            def rstd_(n):
                pool.wait_ge(s_mv, nth(2, n, 2))
                g.tensor_tensor(ve[:, :].unsqueeze(2), mv[:, :].rearrange("p (k a) -> p k a", a=2)[:, :, 1:2],
                                eps[:, :].unsqueeze(2), ALU.add).then_inc(s_ve, 1)
                pool.wait_ge(s_ve, nth(1, n, 1))
                g.tensor_tensor(rstd[:, :], ve[:, :], minus_half[:, 0:TILES], ALU.pow).then_inc(s_rstd, 1)

            def iteration(n):
                nx, m = n + 1, n - 1
                if live(nx):
                    copy_in(nx)
                if live(n):
                    norms(n, 1)
                    scale_q(n, 1, 0)
                    scale_q(n, 1, 1)
                if live(m):
                    residual(m)
                if live(nx):
                    add(nx, 0, 0)
                    add(nx, 0, 1)
                if live(m):
                    rstd_(m)
                if live(nx):
                    add(nx, 0, 2)
                    add(nx, 0, 3)
                    norms(nx, 0)
                    scale_q(nx, 0, 0)
                    scale_q(nx, 0, 1)
                    add(nx, 1, 0)
                    add(nx, 1, 1)
                    add(nx, 1, 2)
                    add(nx, 1, 3)

            iteration(-1)
            iteration(0)
            iteration(1)
            with pool.Fori(2, STEPS - 1) as n:
                iteration(n)
            iteration(STEPS - 1)
            iteration(STEPS)

        @block.scalar
        def _(act):
            a = nc.scalar
            act.wait_ge(s_const, 16 * NCONST)
            act.wait_ge(s_zero, 2)

            def first_attention(s):
                act.wait_ge(s_a["t"], nth(1, s, 1))
                a.activation(ax[:, :], pT[:, 0:LEN], ACT.Copy).then_inc(s_a["x"], 1)
                act.wait_ge(s_a["qkv"], nth(3, s, 1))
                a.activation(aq[:, :], pQ[0][:, 0:LEN], ACT.Identity, bias=abq[:, 0:1]).then_inc(s_a["q"], 1)
                act.wait_ge(s_a["qkv"], nth(3, s, 2))
                a.activation(ak[:, :], pQ[1][:, 0:LEN], ACT.Identity, bias=abq[:, 1:2]).then_inc(s_a["k"], 1)
                act.wait_ge(s_a["neg"], nth(1, s, 1))
                for T in range(TILES):
                    a.activation(ap_[:, T * LEN:(T + 1) * LEN], pS[:, T * LEN:(T + 1) * LEN], ACT.Exp,
                                 scale=float(P) ** -0.5, bias=am2[:, T:T + 1],
                                 accum_out=as2[:, T:T + 1]).then_inc(s_a["exp"], 1)
                act.wait_ge(s_a["pt"], nth(1, s, 1))
                a.activation(apt[:, :], pP[:, :], ACT.Copy).then_inc(s_a["pte"], 1)

            first_attention(0)
            with act.Fori(1, SEQS) as s:
                first_attention(s)

            def shifted(n):
                act.wait_ge(s_xt, nth(1, n, 1))
                act.wait_ge(s_qkv, nth(12, n - 1, 12))
                a.activation(xs[0:64, :], pT[0:64, 0:LEN], ACT.Copy).then_inc(s_xs, 1)
                a.activation(xs[64:P, 1:LEN], pT[64:P, 0:LEN - 1], ACT.Copy).then_inc(s_xs, 1)

            def square(n, T, m):
                i = 4 * T + m
                act.wait_ge(s_qkv, nth(12, n, 6 * T + m + 1))
                act.wait_ge(s_n2, nth(8, n, i - 1))
                a.activation(sq[:, (m % 2) * CH:(m % 2 + 1) * CH], pQ[m % 2][:, :], ACT.Square).then_inc(s_sq, 1)

            def copy_v(n, T, c):
                act.wait_ge(s_qkv, nth(12, n, 6 * T + 5 + c))
                act.wait_ge(s_av, nth(4, n - 1, 2 * T + 2))
                if T == 0:
                    act.wait_ge(s_vb0, nth(32, n - 1, 32))
                else:
                    act.wait_ge(s_vb1, nth(16, n - 1, 16))
                a.activation(v[:, T * INNER + c * CH:T * INNER + (c + 1) * CH], pQ[c][:, :], ACT.Copy)\
                 .then_inc(s_v, 1)

            def take_qk(n, T, g):
                act.wait_ge(s_qt, nth(8, n, 4 * T + g + 1))
                act.wait_ge(s_s, nth(4, n - 1, 4 if T else 3))
                pr = slice(4 * (g % 2), 4 * (g % 2) + 4)
                src = pT[:, :].rearrange("p (a w q) -> p a w q", a=4, w=4)
                if g < 2:
                    for h in range(2):
                        r = slice(64 * h, 64 * h + 64)
                        a.activation(qz5[r, pr, 4 * T:4 * T + 4, h, :], src[r], ACT.Copy).then_inc(s_qte, 1)
                else:
                    a.activation(kt3[:, pr, WIN + T * P:WIN + (T + 1) * P],
                                 pT[:, :].rearrange("p (a t) -> p a t", a=4), ACT.Copy).then_inc(s_qte, 1)

            def exps(n, u):
                act.wait_ge(s_sub, nth(4, n, u + 1))
                e = es[:, (u % 2) * CH:(u % 2 + 1) * CH]
                a.activation(e, e, ACT.Exp, scale=8.0).then_inc(s_exp, 1)

            def take_p(n, u):
                act.wait_ge(s_pt, nth(4, n, u + 1))
                act.wait_ge(s_av, nth(4, n, u - 1))
                src = pP[:, :].rearrange("p (a s c) -> p a s c", a=4, s=2)
                for odd in range(2):
                    for s in range(2):
                        a.activation(pz4[64 * s:64 * s + 64, u % 2, odd::2, s, :],
                                     src[64 * odd:64 * odd + 64, :, s, :], ACT.Copy).then_inc(s_pte, 1)

            def take_o(n, u):
                T, al = u // 2, u % 2
                act.wait_ge(s_av, nth(4, n, u + 1))
                act.wait_ge(s_wo, nth(2, n - 1, T + 1))
                a.activation(ot6[:, :, T, :, al, :], pO[:, :].rearrange("p (a s q) -> p a s q", a=PAIRS, s=2),
                             ACT.Copy).then_inc(s_ot, 1)

            def shifted_f(n):
                act.wait_ge(s_f1, nth(1, n, 1))
                a.activation(xf[0:64, :], pF[0:64, 0:LEN], ACT.Copy).then_inc(s_xf, 1)
                a.activation(xf[64:P, 1:LEN], pF[64:P, 0:LEN - 1], ACT.Copy).then_inc(s_xf, 1)

            def gelu(n, T):
                act.wait_ge(s_gt, nth(2, n, T + 1))
                a.activation(gg[:, :], gt[:, :], ACT.Gelu).then_inc(s_gg, 1)

            def take_h(n, T):
                act.wait_ge(s_f5, nth(2, n, T + 1))
                a.activation(ht[:, 0:2 * P], pF[:, 0:2 * P], ACT.Copy).then_inc(s_ht, 1)
                a.activation(ht[0:HLAST, 2 * P:3 * P], pF[0:HLAST, 2 * P:3 * P], ACT.Copy).then_inc(s_ht, 1)

            def iteration(n):
                nx, m = n + 1, n - 1
                if live(m):
                    take_p(m, 3)
                if live(n):
                    copy_v(n, 1, 0)
                    copy_v(n, 1, 1)
                if live(nx):
                    shifted(nx)
                if live(m - 1):
                    take_h(m - 1, 1)
                if live(n):
                    exps(n, 0)
                if live(m):
                    take_o(m, 3)
                if live(nx):
                    square(nx, 0, 0)
                    square(nx, 0, 1)
                if live(m):
                    shifted_f(m)
                if live(n):
                    take_p(n, 0)
                    take_qk(n, 1, 0)
                    take_qk(n, 1, 1)
                if live(nx):
                    square(nx, 0, 2)
                if live(n):
                    take_qk(n, 1, 2)
                    take_qk(n, 1, 3)
                    exps(n, 1)
                    take_o(n, 0)
                if live(nx):
                    square(nx, 0, 3)
                if live(n):
                    take_p(n, 1)
                    exps(n, 2)
                    take_o(n, 1)
                if live(nx):
                    copy_v(nx, 0, 0)
                    copy_v(nx, 0, 1)
                    square(nx, 1, 0)
                    square(nx, 1, 1)
                if live(m):
                    gelu(m, 0)
                if live(m):
                    take_h(m, 0)
                if live(n):
                    take_p(n, 2)
                if live(nx):
                    take_qk(nx, 0, 0)
                    take_qk(nx, 0, 1)
                    take_qk(nx, 0, 2)
                    square(nx, 1, 2)
                if live(n):
                    exps(n, 3)
                    take_o(n, 2)
                if live(nx):
                    take_qk(nx, 0, 3)
                    square(nx, 1, 3)
                if live(m):
                    gelu(m, 1)

            iteration(-1)
            iteration(0)
            iteration(1)
            with act.Fori(2, STEPS - 1) as n:
                iteration(n)
            iteration(STEPS - 1)
            iteration(STEPS)
            iteration(STEPS + 1)

        @block.vector
        def _(dve):
            d = nc.vector
            d.memset(vb[:, :], 0.0)
            d.memset(pz[:, :], 0.0)
            d.memset(ht[:, :], 1.0)
            dve.wait_ge(s_const, 16 * NCONST)
            d.tensor_copy(identh[:, :], ident[:, :])
            d.tensor_copy(mask[:, :], maskf[:, :]).then_inc(s_zero, 1)
            dve.wait_ge(s_x, 16)

            def stats0(k):
                d.bn_stats(st0[:, bass.ds(k * 6, 6)], acc[:, bass.ds(k * P, P)]).then_inc(s_l0, 1)
                dve.wait_ge(s_l0, nth(2, k, 1))
                d.bn_aggr(mv0[:, bass.ds(k * 2, 2)], st0[:, bass.ds(k * 6, 6)]).then_inc(s_l0, 1)
                dve.wait_ge(s_l0, nth(2, k, 2))

            def norm0(k):
                d.tensor_scalar(x_tok[:, bass.ds(k * P, P)], acc[:, bass.ds(k * P, P)], mv0[:, bass.ds(2 * k, 1)],
                                rs0[:, bass.ds(k, 1)], ALU.subtract, ALU.mult)

            for k in range(SEQS * TILES):
                stats0(k)
            dve.wait_ge(s_const, 16 * NCONST)
            rt = rtab[:, :].rearrange("p (l k t c) -> p l k t c", l=DEPTH, k=4, t=TILES)
            rb = rbase[:, :].rearrange("p (k t c) -> p k t c", k=4, t=TILES)
            sc = scales[:, :].rearrange("p (z l c) -> p z l c", z=2, l=DEPTH)
            HD = DH // 2
            for z in range(2):
                for T in range(TILES):
                    d.tensor_tensor(rt[:, :, 2 * z, T, :], sc[:, z],
                                    rb[:, 2 * z, T, :].unsqueeze(1).to_broadcast([P, DEPTH, DH]), ALU.mult)
                    for h in range(2):
                        last = d.tensor_tensor(
                            rt[:, :, 2 * z + 1, T, h * HD:(h + 1) * HD], sc[:, z, :, (1 - h) * HD:(2 - h) * HD],
                            rb[:, 2 * z + 1, T, h * HD:(h + 1) * HD].unsqueeze(1).to_broadcast([P, DEPTH, HD]),
                            ALU.mult)
            last.then_inc(s_rbase, 1)
            dve.wait_ge(s_rbase, 1)
            dve.wait_ge(s_l0p, 2)
            for s in range(SEQS):
                norm0(2 * s)
                d.tensor_scalar(x_tok[:, (2 * s + 1) * P:(2 * s + 2) * P], acc[:, (2 * s + 1) * P:(2 * s + 2) * P],
                                mv0[:, 4 * s + 2:4 * s + 3], rs0[:, 2 * s + 1:2 * s + 2], ALU.subtract, ALU.mult)\
                 .then_inc(s_xready, 1)

            def first_attention(s):
                dve.wait_ge(s_xready, nth(1, s, 1))
                dve.wait_ge(s_a["t"], nth(1, s - 1, 1))
                d.tensor_copy(axin[:, :], x_tok[:, bass.ds(s * LEN, LEN)]).then_inc(s_a["xin"], 1)
                dve.wait_ge(s_a["qkv"], nth(3, s, 3))
                d.tensor_tensor(av[:, :].rearrange("p (t c) -> p t c", t=TILES),
                                pG[:, 0:LEN].rearrange("p (t c) -> p t c", t=TILES),
                                abv[:, :].unsqueeze(1).to_broadcast([P, TILES, P]), ALU.add).then_inc(s_a["v"], 1)
                dve.wait_ge(s_a["s"], nth(1, s, 1))
                d.tensor_reduce(am2[:, :], pS[:, :].rearrange("p (t k) -> p t k", t=TILES), op=ALU.max, axis=AX.X)\
                 .then_inc(s_a["max"], 1)
                dve.wait_ge(s_a["max"], nth(1, s, 1))
                d.tensor_scalar(am2[:, :], am2[:, :], -float(P) ** -0.5, None, ALU.mult).then_inc(s_a["neg"], 1)
                dve.wait_ge(s_a["exp"], nth(2, s, 2))
                d.reciprocal(ar2[:, :], as2[:, :]).then_inc(s_a["rec"], 1)
                dve.wait_ge(s_a["rec"], nth(1, s, 1))
                dve.wait_ge(s_a["o"], nth(1, s, 1))
                for T in range(TILES):
                    o = acc[:, bass.ds(s * LEN + T * P, P)]
                    last = d.scalar_tensor_tensor(out=o, in0=pO[:, T * P:(T + 1) * P], scalar=ar2[:, T:T + 1],
                                                  in1=o, op0=ALU.mult, op1=ALU.add)
                last.then_inc(s_a["done"], 1)

            first_attention(0)
            with dve.Fori(1, SEQS) as s:
                first_attention(s)

            def rotate(n, T, m):
                i, kind, b = 4 * T + m, 2 * (m // 2), (m % 2) * CH
                dve.wait_ge(s_sq, nth(8, n, i + 1))
                dve.wait_ge(s_add, nth(8, n, i - 1))
                src = heads(pQ[m % 2][:, :])
                d.tensor_tensor(heads(t1[:, b:b + CH]), src, table(n, kind, T), ALU.mult).then_inc(s_t1, 1)
                o2 = heads(t2[:, b:b + CH])
                d.tensor_tensor(o2[:, :, 0:HD], src[:, :, HD:], table(n, kind + 1, T, 0), ALU.mult)
                d.tensor_tensor(o2[:, :, HD:], src[:, :, 0:HD], table(n, kind + 1, T, 1), ALU.mult)\
                 .then_inc(s_rot, 1)
                d.tensor_reduce(n2[:, T * 2 * HEADS + m * CHH:T * 2 * HEADS + (m + 1) * CHH],
                                heads(sq[:, b:b + CH]), op=ALU.add, axis=AX.X).then_inc(s_n2, 1)
                if m == 3:
                    w = slice(T * 2 * HEADS, (T + 1) * 2 * HEADS)
                    dve.wait_ge(s_n2, nth(8, n, i + 1))
                    dve.wait_ge(s_rn, nth(2, n - 1, T + 1))
                    d.tensor_scalar(n2c[:, w], n2[:, w], 1e-24, None, ALU.max).then_inc(s_n2c, 1)

            def scale_k(n, T, m):
                dve.wait_ge(s_add, nth(8, n, 4 * T + m + 1))
                dve.wait_ge(s_rn, nth(2, n, T + 1))
                c = heads(rot[:, (4 * T + m) * CH:(4 * T + m + 1) * CH])
                r = rnorm[:, T * 2 * HEADS + m * CHH:T * 2 * HEADS + (m + 1) * CHH]
                d.tensor_tensor(c, c, over(r, CHH, DH), ALU.mult).then_inc(s_ksc, 1)

            def less_max(n, u):
                dve.wait_ge(s_s, nth(4, n, u + 1))
                src = heads(pS[:, :])
                m = m8[:, (u % 2) * PAIRS:(u % 2 + 1) * PAIRS]
                d.tensor_reduce(m, src, op=ALU.max, axis=AX.X).then_inc(s_max, 1)
                dve.wait_ge(s_max, nth(4, n, u + 1))
                dve.wait_ge(s_pt, nth(4, n, u - 1))
                d.tensor_tensor(heads(es[:, (u % 2) * CH:(u % 2 + 1) * CH]), src, over(m, PAIRS, DH), ALU.subtract)\
                 .then_inc(s_sub, 1)

            def divide(n, u):
                dve.wait_ge(s_exp, nth(4, n, u + 1))
                e = heads(es[:, (u % 2) * CH:(u % 2 + 1) * CH])
                s_, r_ = (t[:, (u % 2) * PAIRS:(u % 2 + 1) * PAIRS] for t in (s8, r8))
                d.tensor_reduce(s_, e, op=ALU.add, axis=AX.X).then_inc(s_sum, 1)
                dve.wait_ge(s_sum, nth(4, n, u + 1))
                d.reciprocal(r_, s_).then_inc(s_rec, 1)
                dve.wait_ge(s_rec, nth(4, n, u + 1))
                d.tensor_tensor(e, e, over(r_, PAIRS, DH), ALU.mult).then_inc(s_p, 1)

            def middle(n, T):
                dve.wait_ge(s_wo, nth(2, n, T + 1))
                dve.wait_ge(s_f1, nth(1, n - 1, 1))
                dve.wait_ge(s_res, nth(1, n - 1, 1))
                d.tensor_tensor(xm[:, T * P:(T + 1) * P], pO[:, 0:P], tokens(x_tok, n, T), ALU.add)\
                 .then_inc(s_mid, 1)

            def stats(n):
                dve.wait_ge(s_f2, nth(1, n, 1))
                for T in range(TILES):
                    d.bn_stats(stat[:, T * 6:(T + 1) * 6], pF[:, T * P:(T + 1) * P]).then_inc(s_st, 1)
                dve.wait_ge(s_zero, 2)
                dve.wait_ge(s_st, nth(2, n, 2))
                for T in range(TILES):
                    d.bn_aggr(mv[:, T * 2:(T + 1) * 2], stat[:, T * 6:(T + 1) * 6]).then_inc(s_mv, 1)

            def normalise(n):
                dve.wait_ge(s_rstd, nth(1, n, 1))
                for T in range(TILES):
                    d.tensor_scalar(xn[:, T * P:(T + 1) * P], pF[:, T * P:(T + 1) * P], mv[:, 2 * T:2 * T + 1],
                                    rstd[:, T:T + 1], ALU.subtract, ALU.mult).then_inc(s_xn, 1)

            def affine(n):
                dve.wait_ge(s_f3, nth(1, n, 1))
                d.tensor_scalar(xg[:, :], pF[:, 0:LEN], gain[:, bass.ds(layer(n), 1)],
                                shift[:, bass.ds(layer(n), 1)], ALU.mult, ALU.add).then_inc(s_xg, 1)

            def bias_gate(n, T):
                dve.wait_ge(s_f4, nth(2, n, T + 1))
                d.tensor_tensor(gt[:, :], pF[:, 0:HID], b_1[:, bass.ds(par(n) * 2 * HID + HID, HID)], ALU.add)\
                 .then_inc(s_gt, 1)
                d.tensor_tensor(am[:, :], pG[:, 0:HID], b_1[:, bass.ds(par(n) * 2 * HID, HID)], ALU.add)\
                 .then_inc(s_am, 1)

            def gated(n, T):
                dve.wait_ge(s_gg, nth(2, n, T + 1))
                dve.wait_ge(s_am, nth(2, n, T + 1))
                d.tensor_tensor(hm[:, :], am[:, :], gg[:, :], ALU.mult).then_inc(s_hm, 1)

            def finish(n, T):
                dve.wait_ge(s_f6, nth(2, n, T + 1))
                dve.wait_ge(s_res, nth(1, n, 1))
                o = tokens(x_tok, n, T)
                d.tensor_tensor(o, pG[:, 0:P], o, ALU.add).then_inc(s_xready if T else s_fin0, 1)

            def iteration(n):
                nx, m = n + 1, n - 1
                if live(n):
                    scale_k(n, 1, 2)
                    scale_k(n, 1, 3)
                    less_max(n, 0)
                if live(m - 1):
                    finish(m - 1, 1)
                if live(m):
                    middle(m, 1)
                if live(nx):
                    rotate(nx, 0, 0)
                if live(n):
                    divide(n, 0)
                if live(nx):
                    rotate(nx, 0, 1)
                if live(m):
                    stats(m)
                if live(n):
                    less_max(n, 1)
                if live(nx):
                    rotate(nx, 0, 2)
                if live(n):
                    divide(n, 1)
                if live(m):
                    normalise(m)
                if live(nx):
                    rotate(nx, 0, 3)
                if live(n):
                    less_max(n, 2)
                if live(m):
                    affine(m)
                if live(nx):
                    rotate(nx, 1, 0)
                if live(m):
                    bias_gate(m, 0)
                if live(n):
                    divide(n, 2)
                    middle(n, 0)
                if live(nx):
                    rotate(nx, 1, 1)
                if live(m):
                    gated(m, 0)
                if live(nx):
                    scale_k(nx, 0, 2)
                    scale_k(nx, 0, 3)
                if live(n):
                    less_max(n, 3)
                if live(nx):
                    rotate(nx, 1, 2)
                if live(m):
                    finish(m, 0)
                if live(n):
                    divide(n, 3)
                if live(nx):
                    rotate(nx, 1, 3)
                if live(m):
                    bias_gate(m, 1)
                    gated(m, 1)

            iteration(-1)
            iteration(0)
            iteration(1)
            with dve.Fori(2, STEPS - 1) as n:
                iteration(n)
            iteration(STEPS - 1)
            iteration(STEPS)
            iteration(STEPS + 1)
            dve.wait_ge(s_xready, STEPS + SEQS)
            dve.wait_ge(s_fin0, STEPS)
            d.tensor_tensor(acc[:, :], acc[:, :], x_tok[:, :], ALU.add).then_inc(s_fin, 1)

        @block.tensor
        def _(pe):
            t = nc.tensor

            def mm(o, l, r, start=True, stop=True):
                return t.matmul(o, l, r, start=start, stop=stop, skip_group_check=True)

            pe.wait_ge(s_const, 16 * NCONST)
            pe.wait_ge(s_zero, 2)

            def first_attention(s):
                pe.wait_ge(s_a["xin"], nth(1, s, 1))
                for T in range(TILES):
                    last = t.transpose(pT[:, T * P:(T + 1) * P], axin[:, T * P:(T + 1) * P], ident[:, :])
                last.then_inc(s_a["t"], 1)
                pe.wait_ge(s_a["x"], nth(1, s, 1))
                mm(pQ[0][:, 0:LEN], aw[:, 0:P], ax[:, :]).then_inc(s_a["qkv"], 1)
                mm(pQ[1][:, 0:LEN], aw[:, P:2 * P], ax[:, :]).then_inc(s_a["qkv"], 1)
                for T in range(TILES):
                    last = mm(pG[:, T * P:(T + 1) * P], ax[:, T * P:(T + 1) * P], aw[:, 2 * P:3 * P])
                last.then_inc(s_a["qkv"], 1)
                pe.wait_ge(s_a["q"], nth(1, s, 1))
                pe.wait_ge(s_a["k"], nth(1, s, 1))
                for T in range(TILES):
                    last = mm(pS[:, T * LEN:(T + 1) * LEN], aq[:, T * P:(T + 1) * P], ak[:, :])
                last.then_inc(s_a["s"], 1)
                pe.wait_ge(s_a["exp"], nth(2, s, 2))
                for k in range(TILES):
                    for T in range(TILES):
                        last = t.transpose(pP[:, (k * TILES + T) * P:(k * TILES + T + 1) * P],
                                           ap_[:, T * LEN + k * P:T * LEN + (k + 1) * P], ident[:, :])
                last.then_inc(s_a["pt"], 1)
                pe.wait_ge(s_a["pte"], nth(1, s, 1))
                pe.wait_ge(s_a["v"], nth(1, s, 1))
                pe.wait_ge(s_a["done"], nth(1, s - 1, 1))
                for T in range(TILES):
                    for k in range(TILES):
                        last = mm(pO[:, T * P:(T + 1) * P], apt[:, (k * TILES + T) * P:(k * TILES + T + 1) * P],
                                  av[:, k * P:(k + 1) * P], start=k == 0, stop=k == TILES - 1)
                last.then_inc(s_a["o"], 1)

            first_attention(0)
            with pe.Fori(1, SEQS) as s:
                first_attention(s)
            pe.wait_ge(s_a["done"], SEQS)
            pe.wait_ge(s_w, 2 * 16 * WLOADS)

            def take_in(n):
                pe.wait_ge(s_xin, nth(1, n, 1))
                pe.wait_ge(s_qte, nth(12, n - 1, 6))
                for T in range(TILES):
                    last = t.transpose(pT[:, T * P:(T + 1) * P], xin[:, T * P:(T + 1) * P], ident[:, :])
                last.then_inc(s_xt, 1)

            def project(n, T, i):
                pe.wait_ge(s_xs, nth(2, n, 2))
                if i == 0 and T == 0:
                    pe.wait_ge(s_w, layer(n) * (16 * WLOADS) + 16 * WLOADS)
                if i >= 2:
                    pe.wait_ge(s_rot, nth(8, n, 4 * T + i - 1))
                elif T:
                    pe.wait_ge(s_v, nth(4, n, i + 1))
                else:
                    pe.wait_ge(s_v, nth(4, n - 1, 2 + i + 1))
                mm(pQ[i % 2][:, :], xs[:, T * P:(T + 1) * P], w_qkv[:, bass.ds(par(n) * QKV + i * CH, CH)])\
                    .then_inc(s_qkv, 1)

            def turn_qk(n, T, g):
                if g < 2:
                    pe.wait_ge(s_qsc, nth(4, n, 2 * T + g + 1))
                else:
                    pe.wait_ge(s_ksc, nth(4, n, 2 * T + g - 1))
                if g == 0 and T == 0:
                    pe.wait_ge(s_qte, nth(12, n - 1, 12))
                elif g == 0:
                    pe.wait_ge(s_qte, nth(12, n, 6))
                    if live(n + 1):
                        pe.wait_ge(s_xs, nth(2, n + 1, 2))
                else:
                    pe.wait_ge(s_qte, nth(12, n, 6 * T + (2 * g if g < 3 else 5)))
                for k in range(4):
                    last = t.transpose(pT[:, k * P:(k + 1) * P],
                                       rot[:, (4 * T + g) * CH + k * P:(4 * T + g) * CH + (k + 1) * P], ident[:, :])
                last.then_inc(s_qt, 1)

            def scores(n, u):
                T, al = u // 2, u % 2
                pe.wait_ge(s_qte, nth(12, n, 6 * T + 6))
                pe.wait_ge(s_sub, nth(4, n, u))
                first = int(u == 0)
                mm(pS[:, :], identh[:, :],
                   mask[:, first * 64:first * 64 + 64].unsqueeze(1).to_broadcast([P, PAIRS, 64]),
                   stop=False)
                for pair in range(PAIRS):
                    for s in range(2):
                        w = 4 * T + al + 2 * s
                        last = mm(pS[64 * s:64 * s + 64, pair * 64:pair * 64 + 64],
                                  qz[:, (pair * 8 + w) * 64:(pair * 8 + w) * 64 + 64],
                                  kt3[:, pair, WIN * w:WIN * w + 64], start=False, stop=pair == PAIRS - 1)
                last.then_inc(s_s, 1)

            def turn_p(n, u):
                pe.wait_ge(s_p, nth(4, n, u + 1))
                pe.wait_ge(s_pte, nth(16, n, 4 * u))
                for k in range(4):
                    c = (u % 2) * CH + k * P
                    last = t.transpose(pP[:, k * P:(k + 1) * P], es[:, c:c + P], ident[:, :])
                last.then_inc(s_pt, 1)

            def values(n, u):
                T, al = u // 2, u % 2
                pe.wait_ge(s_pte, nth(16, n, 4 * u + 4))
                if al:
                    pe.wait_ge(s_v, nth(4, n, 2 * T + 2))
                else:
                    pe.wait_ge(s_vb0, nth(32, n, 32))
                    if T:
                        pe.wait_ge(s_vb1, nth(16, n, 16))
                pe.wait_ge(s_ot, nth(4, n, u))
                if al == 0:
                    pe.wait_ge(s_mid, nth(2, n, T))
                src = v if al else vb
                for h in range(HEADS):
                    pair, hh = h // 2, h % 2
                    last = mm(pO[64 * hh:64 * hh + 64, pair * 64:pair * 64 + 64],
                              src[:, T * INNER + h * DH:T * INNER + (h + 1) * DH],
                              pz5[:, u % 2, pair, :, hh, :])
                last.then_inc(s_av, 1)

            def project_out(n, T):
                pe.wait_ge(s_ot, nth(4, n, 2 * T + 2))
                for pair in range(PAIRS):
                    last = mm(pO[:, 0:P], ot[:, pair * LEN + T * P:pair * LEN + (T + 1) * P],
                              w_o[:, bass.ds(par(n) * (PAIRS * P) + pair * P, P)],
                              start=pair == 0, stop=pair == PAIRS - 1)
                last.then_inc(s_wo, 1)

            def turn_to_pF(src, signal):
                for T in range(TILES):
                    last = t.transpose(pF[:, T * P:(T + 1) * P], src[:, T * P:(T + 1) * P], ident[:, :])
                last.then_inc(signal, 1)

            def hidden(n, T):
                pe.wait_ge(s_xg, nth(1, n, 1))
                if T:
                    pe.wait_ge(s_ht, nth(4, n, 2))
                    pe.wait_ge(s_fin0, nth(1, n, 1))
                else:
                    pe.wait_ge(s_xready, nth(1, n - 1, SEQS + 1))
                l = xg[:, T * P:(T + 1) * P]
                mm(pF[:, 0:HID], l, w_1[:, bass.ds(par(n) * 2 * HID + HID, HID)])
                mm(pG[:, 0:HID], l, w_1[:, bass.ds(par(n) * 2 * HID, HID)]).then_inc(s_f4, 1)

            def turn_h(n, T):
                pe.wait_ge(s_hm, nth(2, n, T + 1))
                for j in range(HCH):
                    w = P if j < 2 else HLAST
                    last = t.transpose(pF[0:w, j * P:(j + 1) * P], hm[:, j * P:j * P + w], ident[:, :])
                last.then_inc(s_f5, 1)

            def down(n, T):
                pe.wait_ge(s_ht, nth(4, n, 2 * T + 2))
                for j in range(HCH):
                    k = P if j < 2 else HLAST + 1
                    last = mm(pG[:, 0:P], ht[0:k, j * P:(j + 1) * P],
                              w_2[0:k, bass.ds(par(n) * (HCH * P) + j * P, P)], start=j == 0, stop=j == HCH - 1)
                last.then_inc(s_f6, 1)

            def iteration(n):
                nx, m = n + 1, n - 1
                if live(m):
                    turn_p(m, 3)
                if live(n):
                    project(n, 1, 4)
                    project(n, 1, 5)
                if live(nx):
                    take_in(nx)
                if live(m - 1):
                    turn_h(m - 1, 1)
                if live(n):
                    scores(n, 0)
                if live(m):
                    values(m, 3)
                if live(m - 1):
                    down(m - 1, 1)
                if live(nx):
                    project(nx, 0, 0)
                if live(m):
                    project_out(m, 1)
                if live(nx):
                    project(nx, 0, 1)
                if live(m):
                    pe.wait_ge(s_mid, nth(2, m, 2))
                    turn_to_pF(xm, s_f1)
                if live(n):
                    turn_p(n, 0)
                    turn_qk(n, 1, 0)
                    turn_qk(n, 1, 1)
                if live(m):
                    pe.wait_ge(s_xf, nth(2, m, 2))
                    turn_to_pF(xf, s_f2)
                if live(nx):
                    project(nx, 0, 2)
                if live(n):
                    turn_qk(n, 1, 2)
                    scores(n, 1)
                    turn_qk(n, 1, 3)
                    values(n, 0)
                if live(nx):
                    project(nx, 0, 3)
                if live(m):
                    pe.wait_ge(s_xn, nth(2, m, 2))
                    turn_to_pF(xn, s_f3)
                if live(n):
                    turn_p(n, 1)
                    scores(n, 2)
                if live(m):
                    hidden(m, 0)
                if live(n):
                    values(n, 1)
                if live(nx):
                    project(nx, 0, 4)
                    project(nx, 0, 5)
                if live(n):
                    project_out(n, 0)
                if live(nx):
                    project(nx, 1, 0)
                    project(nx, 1, 1)
                if live(m):
                    turn_h(m, 0)
                if live(n):
                    turn_p(n, 2)
                if live(nx):
                    turn_qk(nx, 0, 0)
                    turn_qk(nx, 0, 1)
                if live(m):
                    down(m, 0)
                if live(n):
                    scores(n, 3)
                if live(nx):
                    turn_qk(nx, 0, 2)
                    project(nx, 1, 2)
                if live(n):
                    values(n, 2)
                if live(nx):
                    turn_qk(nx, 0, 3)
                    project(nx, 1, 3)
                if live(m):
                    hidden(m, 1)

            iteration(-1)
            iteration(0)
            iteration(1)
            with pe.Fori(2, STEPS - 1) as n:
                iteration(n)
            iteration(STEPS - 1)
            iteration(STEPS)
            iteration(STEPS + 1)


def constants():
    f = np.float32
    half = np.arange(0, DH, 2, dtype=f)
    inv_freq = (f(1.0) / np.power(f(10000.0), half / f(DH))).astype(f)
    t = np.arange(LEN, dtype=f)
    freqs = (t[:, None] * inv_freq[None, :]).astype(f)
    base = ((half + f(0.4 * DH)) / f(1.4 * DH)).astype(f)
    power = (t - f(LEN // 2)) / f(WIN // 2)
    scale = np.power(base[None, :], power[:, None]).astype(f)
    cos, sin = np.cos(freqs), np.sin(freqs)
    rows = []
    for s in (scale, f(1.0) / scale):
        rows.append(np.concatenate([cos * s, cos * s], 1))
        rows.append(np.concatenate([-sin * s, sin * s], 1))
    rot_base = np.stack(rows).reshape(4, TILES, P, DH).transpose(2, 0, 1, 3).reshape(P, -1).astype(f)
    q = np.arange(P) % WIN
    j = np.arange(2 * WIN)
    seen = np.where(j[None, :] < WIN, q[:, None] <= j[None, :], j[None, :] - WIN <= q[:, None])
    first = seen & ((np.arange(P)[:, None] >= 64) | (j[None, :] >= WIN))
    masks = np.where(np.concatenate([seen, first], 1), 0.0, MASKED).astype(f)
    return {"rot_base": rot_base, "masks": masks, "ident_f": np.eye(P, dtype=f)}


_INS = ["X", "W_q", "W_k", "W_v", "b_q", "b_k", "b_v"]
_FFN = ["Wqkv", "q_scale", "k_scale", "Wo", "ln_g", "ln_b", "W1", "b1", "W2", "b2"]
_FLAT = {"Wqkv": (DEPTH * P, QKV), "Wo": (DEPTH * INNER, P), "W1": (DEPTH * P, 2 * HID), "W2": (DEPTH * HID, P)}


def kernel(**inputs):
    import concourse.bacc as _bacc
    from concourse.bass_utils import run_bass_kernel_spmd as _run

    nc = _bacc.Bacc("TRN2", target_bir_lowering=False, num_devices=1)
    arrays = {}
    for n in _INS:
        arrays[n] = np.ascontiguousarray(inputs["L0_attn_" + n])
    for n in _FFN:
        a = np.ascontiguousarray(inputs["L0_ffn_" + n])
        arrays[n] = a.reshape(_FLAT[n]) if n in _FLAT else a
    arrays.update(constants())
    arrays = {f"in_{n}": a for n, a in arrays.items()}
    args = [nc.dram_tensor(n, a.shape, mybir.dt.from_np(a.dtype), kind="ExternalInput").ap()
            for n, a in arrays.items()]
    out = nc.dram_tensor("out", (SEQS, LEN, P), F32, kind="ExternalOutput").ap()
    program(nc, *args, out)
    r = _run(nc, [arrays], core_ids=[0])
    return r.results[0]["out"]
```

```python
from contextlib import ExitStack

import concourse.bass as bass
import numpy as np
from concourse import mybir

F32 = mybir.dt.float32
BF16 = mybir.dt.bfloat16
ALU = mybir.AluOpType
ACT = mybir.ActivationFunctionType
AX = mybir.AxisListType

P = 128
SEQS, LEN = 8, 256
TILES = LEN // P
DEPTH, HEADS, DH, WIN = 6, 16, 64, 32
INNER = HEADS * DH
PAIRS = HEADS // 2
HID = int(P * 4 * 2 / 3)
HCH = 3
HLAST = HID - 2 * P
STEPS = DEPTH * SEQS
CH = 512
CHH = CH // DH
QKV = 3 * INNER
WLOADS = 8
MASKED = -1.0e30
FIRST, LAST = 2, STEPS - 2
EPS = 1e-5


def nth(per, n, e):
    value = n * per + e
    if isinstance(value, int):
        return max(0, value)
    assert value.min_val > 0
    return value


def live(n):
    return not isinstance(n, int) or 0 <= n < STEPS


def program(nc, X, Wq, Wk, Wv, bq, bk, bv, Wqkv, q_scale, k_scale, Wo, ln_g, ln_b, W1, b1, W2, b2,
            rot_base, masks, ident_f, out):
    ctx = ExitStack()
    with ctx:
        def sb(name, cols, dt=F32):
            return ctx.enter_context(nc.sbuf_tensor(name, [P, cols], dt))

        def sem(name):
            return ctx.enter_context(nc.semaphore(name))

        ident = sb("ident", P)
        identh = sb("identh", P, BF16)
        mask = sb("mask", 2 * 64, BF16)
        maskf = sb("maskf", 2 * 64)
        x_tok = sb("x_tok", SEQS * TILES * P)
        acc = sb("acc", SEQS * TILES * P)
        w_qkv = sb("w_qkv", 2 * QKV)
        w_o = sb("w_o", 2 * PAIRS * P)
        w_1 = sb("w_1", 2 * 2 * HID)
        w_2 = sb("w_2", 2 * HCH * P)
        b_1 = sb("b_1", 2 * 2 * HID)
        gain = sb("gain", DEPTH)
        shift = sb("shift", DEPTH)
        rbase = sb("rbase", 4 * TILES * DH)
        scales = sb("scales", 2 * DEPTH * DH)
        rtab = sb("rtab", DEPTH * 4 * TILES * DH)
        xin = sb("xin", TILES * P)
        xs = sb("xs", LEN)
        sq = sb("sq", 2 * CH)
        t1 = sb("t1", 2 * CH)
        t2 = sb("t2", 2 * CH)
        rot = sb("rot", TILES * 4 * CH)
        n2 = sb("n2", TILES * 2 * HEADS)
        n2c = sb("n2c", TILES * 2 * HEADS)
        rnorm = sb("rnorm", TILES * 2 * HEADS)
        minus_half = sb("minus_half", HEADS)
        eps = sb("eps", TILES)
        qz = sb("qz", PAIRS * 8 * 64)
        kt = sb("kt", PAIRS * (WIN + LEN))
        v = sb("v", TILES * INNER)
        vb = sb("vb", TILES * INNER)
        es = sb("es", 2 * CH)
        m8 = sb("m8", 2 * PAIRS)
        s8 = sb("s8", 2 * PAIRS)
        r8 = sb("r8", 2 * PAIRS)
        pz = sb("pz", 2 * PAIRS * P)
        ot = sb("ot", PAIRS * LEN)
        xm = sb("xm", TILES * P)
        xf = sb("xf", LEN)
        stat = sb("stat", TILES * 6)
        mv = sb("mv", TILES * 2)
        ve = sb("ve", TILES)
        rstd = sb("rstd", TILES)
        xn = sb("xn", TILES * P)
        xg = sb("xg", LEN)
        gt = sb("gt", TILES * HID)
        am = sb("am", TILES * HID)
        ht = sb("ht", TILES * HCH * P)
        aw = sb("aw", 3 * P)
        abq = sb("abq", 2)
        abv = sb("abv", P)
        st0 = sb("st0", SEQS * TILES * 6)
        mv0 = sb("mv0", SEQS * TILES * 2)
        ve0 = sb("ve0", SEQS * TILES)
        rs0 = sb("rs0", SEQS * TILES)
        axin = sb("axin", LEN)
        ax = sb("ax", LEN)
        aq = sb("aq", LEN)
        ak = sb("ak", LEN)
        av = sb("av", LEN)
        am2 = sb("am2", TILES)
        ap_ = sb("ap_", TILES * LEN)
        as2 = sb("as2", TILES)
        ar2 = sb("ar2", TILES)
        apt = sb("apt", TILES * LEN)

        bank = [ctx.enter_context(nc.psum_tensor(f"bank{i}", [P, CH], F32)) for i in range(8)]
        pQ = bank[0:2]
        pT, pS, pP, pO, pF, pG = bank[2:8]
        pH = (pG, pF)

        s_const = sem("s_const")
        s_x = sem("s_x")
        s_w = sem("s_w")
        s_zero = sem("s_zero")
        s_rbase = sem("s_rbase")
        s_xready = sem("s_xready")
        s_xin = sem("s_xin")
        s_xt = sem("s_xt")
        s_xs = sem("s_xs")
        s_qkv = sem("s_qkv")
        s_sq = sem("s_sq")
        s_t1 = sem("s_t1")
        s_rot = sem("s_rot")
        s_n2 = sem("s_n2")
        s_add = sem("s_add")
        s_n2c = sem("s_n2c")
        s_rn = sem("s_rn")
        s_qsc = sem("s_qsc")
        s_ksc = sem("s_ksc")
        s_qt = sem("s_qt")
        s_qte = sem("s_qte")
        s_v = sem("s_v")
        s_vb0 = sem("s_vb0")
        s_vb1 = sem("s_vb1")
        s_s = sem("s_s")
        s_max = sem("s_max")
        s_sub = sem("s_sub")
        s_exp = sem("s_exp")
        s_sum = sem("s_sum")
        s_rec = sem("s_rec")
        s_p = sem("s_p")
        s_pt = sem("s_pt")
        s_pte = sem("s_pte")
        s_av = sem("s_av")
        s_ot = sem("s_ot")
        s_wo = sem("s_wo")
        s_mid = sem("s_mid")
        s_res = sem("s_res")
        s_f1 = sem("s_f1")
        s_xf = sem("s_xf")
        s_f2 = sem("s_f2")
        s_st = sem("s_st")
        s_mv = sem("s_mv")
        s_ve = sem("s_ve")
        s_rstd = sem("s_rstd")
        s_xn = sem("s_xn")
        s_f3 = sem("s_f3")
        s_xg = sem("s_xg")
        s_f4g = sem("s_f4g")
        s_gt = sem("s_gt")
        s_gg = sem("s_gg")
        s_f4a = sem("s_f4a")
        s_am = sem("s_am")
        s_hm = sem("s_hm")
        s_f5 = sem("s_f5")
        s_ht = sem("s_ht")
        s_f6 = sem("s_f6")
        s_l0 = sem("s_l0")
        s_l0p = sem("s_l0p")
        s_a = {k: sem("s_a_" + k) for k in ("xin", "t", "x", "qkv", "q", "k", "v", "s", "max", "neg", "exp",
                                            "rec", "pt", "pte", "o", "done")}
        s_fin = sem("s_fin")
        s_out = sem("s_out")

        def layer(n):
            return n // SEQS

        def par(n):
            return (n // SEQS) % 2

        def tokens(t, n, T, k=1):
            return t[:, bass.ds((n % SEQS) * (TILES * P) + T * P, k * P)]

        def heads(a):
            return a.rearrange("p (h c) -> p h c", c=DH)

        def table(n, kind, T, half=None):
            off = layer(n) * (4 * TILES * DH) + (kind * TILES + T) * DH
            w = DH
            if half is not None:
                off, w = off + half * (DH // 2), DH // 2
            return rtab[:, bass.ds(off, w)].unsqueeze(1).to_broadcast([P, CHH, w])

        def over(a, k, w):
            return a.unsqueeze(2).to_broadcast([P, k, w])

        qz5 = qz[:, :].rearrange("p (a w h q) -> p a w h q", a=PAIRS, w=8, h=2)
        kt3 = kt[:, :].rearrange("p (a t) -> p a t", a=PAIRS)
        pz4 = pz[:, :].rearrange("p (b a s c) -> p b a s c", b=2, a=PAIRS, s=2)
        pz5 = pz[:, :].rearrange("p (b a s h q) -> p b a s h q", b=2, a=PAIRS, s=2, h=2)
        ot6 = ot[:, :].rearrange("p (a t s l q) -> p a t s l q", a=PAIRS, t=TILES, s=2, l=2)

        block = ctx.enter_context(nc.Block())

        def chunk_of(i):
            return i * CH, (i if i < 4 else None)

        @block.sync
        def _(sp):
            sp.dma_start(acc[:, :].rearrange("p (s t c) -> p s t c", s=SEQS, t=TILES),
                         X.rearrange("s (t p) c -> p s t c", p=P)).then_inc(s_x, 16)
            for dst, src in ((ident[:, :], ident_f), (maskf[:, :], masks),
                             (rbase[:, :], rot_base),
                             (aw[:, 0:P], Wq), (aw[:, P:2 * P], Wk), (aw[:, 2 * P:3 * P], Wv),
                             (abq[:, 0:1], bq.rearrange("(p a) -> p a", a=1)),
                             (abq[:, 1:2], bk.rearrange("(p a) -> p a", a=1)),
                             (abv[:, :], bv.partition_broadcast(P)),
                             (scales[:, 0:DEPTH * DH], q_scale.rearrange("l c -> (l c)").partition_broadcast(P)),
                             (scales[:, DEPTH * DH:], k_scale.rearrange("l c -> (l c)").partition_broadcast(P)),
                             ):
                sp.dma_start(dst, src).then_inc(s_const, 16)
            for dst, src in ((gain, ln_g), (shift, ln_b)):
                sp.dma_start(dst[:, :], src.rearrange("l c -> c l"), allow_slow_non_contiguous=True)\
                  .then_inc(s_const, 16)

            def weights(l):
                p = l % 2
                sp.dma_start(w_qkv[:, bass.ds(p * QKV, QKV)], Wqkv[bass.ds(l * P, P), :]).then_inc(s_w, 16)
                sp.dma_start(w_o[:, bass.ds(p * PAIRS * P, PAIRS * P)].rearrange("p (a c) -> p a c", a=PAIRS),
                             Wo[bass.ds(l * INNER, INNER), :].rearrange("(a p) c -> p a c", p=P)).then_inc(s_w, 16)
                sp.dma_start(w_1[:, bass.ds(p * 2 * HID, 2 * HID)], W1[bass.ds(l * P, P), :]).then_inc(s_w, 16)
                for j in range(HCH):
                    rows = P if j < 2 else HLAST
                    sp.dma_start(w_2[0:rows, bass.ds(p * HCH * P + j * P, P)],
                                 W2[bass.ds(l * HID + j * P, rows), :]).then_inc(s_w, 16)
                sp.dma_start(w_2[HLAST:HLAST + 1, bass.ds(p * HCH * P + 2 * P, P)], b2[bass.ds(l, 1), :])\
                  .then_inc(s_w, 16)
                sp.dma_start(b_1[:, bass.ds(p * 2 * HID, 2 * HID)],
                             b1[bass.ds(l, 1), :].to_broadcast([P, 2 * HID])).then_inc(s_w, 16)

            weights(0)
            weights(1)

            def copy_v(n):
                sp.wait_ge(s_v, nth(4, n, 3))
                sp.dma_start(vb[WIN:P, 0:INNER], v[0:P - WIN, 0:INNER]).then_inc(s_vb0, 16)
                sp.wait_ge(s_ot, nth(4, n, 0))
                if isinstance(n, int) and n == 0:
                    sp.wait_ge(s_v, 4)
                sp.dma_start(vb[0:WIN, INNER:], v[P - WIN:P, 0:INNER]).then_inc(s_vb1, 16)
                sp.dma_start(vb[WIN:P, INNER:], v[0:P - WIN, INNER:]).then_inc(s_vb1, 16)

            sp.wait_ge(s_zero, 2)
            copy_v(0)
            with sp.Fori(1, SEQS) as n:
                copy_v(n)
            for l in range(1, DEPTH):
                for n in range(l * SEQS, l * SEQS + 3):
                    copy_v(n)
                if l < DEPTH - 1:
                    sp.wait_ge(s_xready, l * SEQS + SEQS)
                    weights(l + 1)
                with sp.Fori(l * SEQS + 3, (l + 1) * SEQS) as n:
                    copy_v(n)
            sp.wait_ge(s_fin, 1)
            sp.dma_start(out.rearrange("s (t p) c -> p s t c", p=P),
                         acc[:, :].rearrange("p (s t c) -> p s t c", s=SEQS, t=TILES)).then_inc(s_out, 16)
            sp.wait_ge(s_out, 16)

        NCONST = 13

        @block.gpsimd
        def _(pool):
            g = nc.gpsimd
            g.memset(minus_half[:, :], -0.5)
            g.memset(eps[:, :], EPS)
            g.memset(qz[:, :], 0.0)
            g.memset(kt[:, :], 0.0)
            g.memset(xs[:, :], 0.0)
            g.memset(xf[:, :], 0.0).then_inc(s_zero, 1)
            pool.wait_ge(s_l0, 2 * SEQS * TILES)
            g.tensor_scalar(ve0[:, :].unsqueeze(2), mv0[:, :].rearrange("p (k a) -> p k a", a=2)[:, :, 1:2],
                            EPS, 1.0, ALU.add, ALU.mult).then_inc(s_l0p, 1)
            pool.wait_ge(s_l0p, 1)
            g.tensor_tensor(rs0[:, :], ve0[:, :], minus_half[:, 0:SEQS * TILES], ALU.pow).then_inc(s_l0p, 1)

            def copy_in(n):
                pool.wait_ge(s_xready, nth(1, n, 1))
                pool.wait_ge(s_xt, nth(1, n - 1, 1))
                g.tensor_copy(xin[:, :], tokens(x_tok, n, 0, TILES)).then_inc(s_xin, 1)

            def add(n, T, m):
                i = 4 * T + m
                pool.wait_ge(s_rot, nth(8, n, i + 1))
                pool.wait_ge(s_qt, nth(8, n - 1, 4 * T + 4))
                b = (m % 2) * CH
                g.tensor_tensor(rot[:, i * CH:(i + 1) * CH], t1[:, b:b + CH], t2[:, b:b + CH], ALU.add)\
                 .then_inc(s_add, 1)

            def norms(n, T, k):
                w = slice((2 * T + k) * HEADS, (2 * T + k + 1) * HEADS)
                pool.wait_ge(s_n2c, nth(4, n, 2 * T + k + 1))
                if k:
                    pool.wait_ge(s_ksc, nth(4, n - 1, 2 * T + 2))
                g.tensor_tensor(rnorm[:, w], n2c[:, w], minus_half[:, :], ALU.pow).then_inc(s_rn, 1)

            def scale_q(n, T, m):
                pool.wait_ge(s_add, nth(8, n, 4 * T + m + 1))
                pool.wait_ge(s_rn, nth(4, n, 2 * T + 1))
                c = heads(rot[:, (4 * T + m) * CH:(4 * T + m + 1) * CH])
                r = rnorm[:, T * 2 * HEADS + m * CHH:T * 2 * HEADS + (m + 1) * CHH]
                g.tensor_tensor(c, c, over(r, CHH, DH), ALU.mult).then_inc(s_qsc, 1)

            def residual(n):
                pool.wait_ge(s_mid, nth(2, n, 2))
                g.tensor_copy(tokens(x_tok, n, 0, TILES), xm[:, :]).then_inc(s_res, 1)

            def rstd_(n):
                pool.wait_ge(s_mv, nth(2, n, 2))
                g.tensor_tensor(ve[:, :].unsqueeze(2), mv[:, :].rearrange("p (k a) -> p k a", a=2)[:, :, 1:2],
                                eps[:, :].unsqueeze(2), ALU.add).then_inc(s_ve, 1)
                pool.wait_ge(s_ve, nth(1, n, 1))
                g.tensor_tensor(rstd[:, :], ve[:, :], minus_half[:, 0:TILES], ALU.pow).then_inc(s_rstd, 1)

            def iteration(n):
                nx, m = n + 1, n - 1
                if live(n):
                    add(n, 1, 3)
                    norms(n, 1, 1)
                    scale_q(n, 1, 0)
                    scale_q(n, 1, 1)
                if live(nx):
                    add(nx, 0, 0)
                    add(nx, 0, 1)
                if live(m):
                    residual(m)
                if live(nx):
                    norms(nx, 0, 0)
                    add(nx, 0, 2)
                if live(m):
                    rstd_(m)
                if live(nx):
                    scale_q(nx, 0, 0)
                    add(nx, 0, 3)
                    norms(nx, 0, 1)
                    scale_q(nx, 0, 1)
                    add(nx, 1, 0)
                    add(nx, 1, 1)
                    norms(nx, 1, 0)
                    if live(nx + 1):
                        copy_in(nx + 1)
                    add(nx, 1, 2)

            copy_in(0)
            for n in range(-1, FIRST):
                iteration(n)
            with pool.Fori(FIRST, LAST) as n:
                iteration(n)
            for n in range(LAST, STEPS + 2):
                iteration(n)

        @block.scalar
        def _(act):
            a = nc.scalar
            act.wait_ge(s_const, 16 * NCONST)
            act.wait_ge(s_zero, 2)

            def first_attention(s):
                act.wait_ge(s_a["t"], nth(1, s, 1))
                a.activation(ax[:, :], pT[:, 0:LEN], ACT.Copy).then_inc(s_a["x"], 1)
                act.wait_ge(s_a["qkv"], nth(3, s, 1))
                a.activation(aq[:, :], pQ[0][:, 0:LEN], ACT.Identity, bias=abq[:, 0:1]).then_inc(s_a["q"], 1)
                act.wait_ge(s_a["qkv"], nth(3, s, 2))
                a.activation(ak[:, :], pQ[1][:, 0:LEN], ACT.Identity, bias=abq[:, 1:2]).then_inc(s_a["k"], 1)
                act.wait_ge(s_a["neg"], nth(1, s, 1))
                for T in range(TILES):
                    a.activation(ap_[:, T * LEN:(T + 1) * LEN], pS[:, T * LEN:(T + 1) * LEN], ACT.Exp,
                                 scale=float(P) ** -0.5, bias=am2[:, T:T + 1],
                                 accum_out=as2[:, T:T + 1]).then_inc(s_a["exp"], 1)
                act.wait_ge(s_a["pt"], nth(1, s, 1))
                a.activation(apt[:, :], pP[:, :], ACT.Copy).then_inc(s_a["pte"], 1)

            first_attention(0)
            with act.Fori(1, SEQS) as s:
                first_attention(s)

            def shifted(n, T):
                act.wait_ge(s_xt, nth(1, n, 1))
                act.wait_ge(s_qkv, nth(12, n - 1, 6 * T + 6))
                a.activation(xs[0:64, T * P:(T + 1) * P], pT[0:64, T * P:(T + 1) * P], ACT.Copy).then_inc(s_xs, 1)
                lo = max(1, T * P)
                a.activation(xs[64:P, lo:(T + 1) * P], pT[64:P, lo - 1:(T + 1) * P - 1], ACT.Copy)\
                 .then_inc(s_xs, 1)

            def square(n, T, m):
                i = 4 * T + m
                act.wait_ge(s_qkv, nth(12, n, 6 * T + m + 1))
                act.wait_ge(s_n2, nth(8, n, i - 1))
                a.activation(sq[:, (m % 2) * CH:(m % 2 + 1) * CH], pQ[m % 2][:, :], ACT.Square).then_inc(s_sq, 1)

            def copy_v(n, T, c):
                act.wait_ge(s_qkv, nth(12, n, 6 * T + 5 + c))
                act.wait_ge(s_av, nth(4, n - 1, 2 * T + 1))
                act.wait_ge(s_vb1, nth(32, n - 1, 32))
                if T == 0:
                    act.wait_ge(s_vb0, nth(16, n - 1, 16))
                a.activation(v[:, T * INNER + c * CH:T * INNER + (c + 1) * CH], pQ[c][:, :], ACT.Copy)\
                 .then_inc(s_v, 1)

            def take_qk(n, T, g):
                act.wait_ge(s_qt, nth(8, n, 4 * T + g + 1))
                act.wait_ge(s_s, nth(4, n - 1, 2 if T == 0 and g < 2 else 4))
                pr = slice(4 * (g % 2), 4 * (g % 2) + 4)
                src = pT[:, :].rearrange("p (a w q) -> p a w q", a=4, w=4)
                if g < 2:
                    for h in range(2):
                        r = slice(64 * h, 64 * h + 64)
                        a.activation(qz5[r, pr, 4 * T:4 * T + 4, h, :], src[r], ACT.Copy).then_inc(s_qte, 1)
                else:
                    a.activation(kt3[:, pr, WIN + T * P:WIN + (T + 1) * P],
                                 pT[:, :].rearrange("p (a t) -> p a t", a=4), ACT.Copy).then_inc(s_qte, 1)

            def exps(n, u):
                act.wait_ge(s_sub, nth(4, n, u + 1))
                e = es[:, (u % 2) * CH:(u % 2 + 1) * CH]
                a.activation(e, e, ACT.Exp, scale=8.0).then_inc(s_exp, 1)

            def take_p(n, u):
                act.wait_ge(s_pt, nth(4, n, u + 1))
                act.wait_ge(s_av, nth(4, n, u - 1))
                src = pP[:, :].rearrange("p (a s c) -> p a s c", a=4, s=2)
                for odd in range(2):
                    for s in range(2):
                        a.activation(pz4[64 * s:64 * s + 64, u % 2, odd::2, s, :],
                                     src[64 * odd:64 * odd + 64, :, s, :], ACT.Copy).then_inc(s_pte, 1)

            def take_o(n, u):
                T, al = u // 2, 1 - u % 2
                act.wait_ge(s_av, nth(4, n, u + 1))
                act.wait_ge(s_wo, nth(2, n - 1, T + 1))
                a.activation(ot6[:, :, T, :, al, :], pO[:, :].rearrange("p (a s q) -> p a s q", a=PAIRS, s=2),
                             ACT.Copy).then_inc(s_ot, 1)

            def shifted_f(n):
                act.wait_ge(s_f1, nth(1, n, 1))
                a.activation(xf[0:64, :], pF[0:64, 0:LEN], ACT.Copy).then_inc(s_xf, 1)
                a.activation(xf[64:P, 1:LEN], pF[64:P, 0:LEN - 1], ACT.Copy).then_inc(s_xf, 1)

            def gelu(n):
                act.wait_ge(s_gt, nth(2, n, 2))
                a.activation(gt[:, :], gt[:, :], ACT.Gelu).then_inc(s_gg, 1)

            def take_h(n):
                act.wait_ge(s_f5, nth(1, n, 1))
                for T in range(TILES):
                    o = T * HCH * P
                    a.activation(ht[:, o:o + 2 * P], pH[T][:, 0:2 * P], ACT.Copy).then_inc(s_ht, 1)
                    a.activation(ht[0:HLAST, o + 2 * P:o + 3 * P], pH[T][0:HLAST, 2 * P:3 * P], ACT.Copy)\
                     .then_inc(s_ht, 1)

            def iteration(n):
                nx, m = n + 1, n - 1
                if live(nx):
                    shifted(nx, 0)
                if live(m):
                    take_p(m, 3)
                if live(n):
                    copy_v(n, 1, 0)
                    copy_v(n, 1, 1)
                if live(nx):
                    shifted(nx, 1)
                if live(n):
                    exps(n, 0)
                if live(nx):
                    square(nx, 0, 0)
                if live(m):
                    take_o(m, 3)
                if live(m - 1):
                    take_h(m - 1)
                if live(nx):
                    square(nx, 0, 1)
                if live(n):
                    take_p(n, 0)
                    take_qk(n, 1, 0)
                    exps(n, 1)
                    take_qk(n, 1, 1)
                if live(nx):
                    square(nx, 0, 2)
                if live(n):
                    take_o(n, 0)
                if live(m):
                    shifted_f(m)
                if live(n):
                    take_qk(n, 1, 2)
                if live(nx):
                    square(nx, 0, 3)
                if live(n):
                    take_qk(n, 1, 3)
                    take_p(n, 1)
                if live(nx):
                    copy_v(nx, 0, 0)
                    copy_v(nx, 0, 1)
                if live(n):
                    exps(n, 2)
                if live(nx):
                    square(nx, 1, 0)
                if live(n):
                    take_o(n, 1)
                if live(nx):
                    square(nx, 1, 1)
                if live(n):
                    take_p(n, 2)
                if live(nx):
                    take_qk(nx, 0, 0)
                if live(n):
                    exps(n, 3)
                if live(nx):
                    take_qk(nx, 0, 1)
                    square(nx, 1, 2)
                if live(n):
                    take_o(n, 2)
                if live(nx):
                    take_qk(nx, 0, 2)
                if live(m):
                    gelu(m)
                if live(nx):
                    square(nx, 1, 3)
                    take_qk(nx, 0, 3)

            for n in range(-1, FIRST):
                iteration(n)
            with act.Fori(FIRST, LAST) as n:
                iteration(n)
            for n in range(LAST, STEPS + 2):
                iteration(n)

        @block.vector
        def _(dve):
            d = nc.vector
            d.memset(vb[:, :], 0.0)
            d.memset(pz[:, :], 0.0)
            d.memset(ht[:, :], 1.0)
            dve.wait_ge(s_const, 16 * NCONST)
            d.tensor_copy(identh[:, :], ident[:, :])
            d.tensor_copy(mask[:, :], maskf[:, :]).then_inc(s_zero, 1)
            dve.wait_ge(s_x, 16)

            def stats0(k):
                d.bn_stats(st0[:, bass.ds(k * 6, 6)], acc[:, bass.ds(k * P, P)]).then_inc(s_l0, 1)
                dve.wait_ge(s_l0, nth(2, k, 1))
                d.bn_aggr(mv0[:, bass.ds(k * 2, 2)], st0[:, bass.ds(k * 6, 6)]).then_inc(s_l0, 1)
                dve.wait_ge(s_l0, nth(2, k, 2))

            def norm0(k):
                d.tensor_scalar(x_tok[:, bass.ds(k * P, P)], acc[:, bass.ds(k * P, P)], mv0[:, bass.ds(2 * k, 1)],
                                rs0[:, bass.ds(k, 1)], ALU.subtract, ALU.mult)

            for k in range(SEQS * TILES):
                stats0(k)
            dve.wait_ge(s_const, 16 * NCONST)
            rt = rtab[:, :].rearrange("p (l k t c) -> p l k t c", l=DEPTH, k=4, t=TILES)
            rb = rbase[:, :].rearrange("p (k t c) -> p k t c", k=4, t=TILES)
            sc = scales[:, :].rearrange("p (z l c) -> p z l c", z=2, l=DEPTH)
            HD = DH // 2
            for z in range(2):
                for T in range(TILES):
                    d.tensor_tensor(rt[:, :, 2 * z, T, :], sc[:, z],
                                    rb[:, 2 * z, T, :].unsqueeze(1).to_broadcast([P, DEPTH, DH]), ALU.mult)
                    for h in range(2):
                        last = d.tensor_tensor(
                            rt[:, :, 2 * z + 1, T, h * HD:(h + 1) * HD], sc[:, z, :, (1 - h) * HD:(2 - h) * HD],
                            rb[:, 2 * z + 1, T, h * HD:(h + 1) * HD].unsqueeze(1).to_broadcast([P, DEPTH, HD]),
                            ALU.mult)
            last.then_inc(s_rbase, 1)
            dve.wait_ge(s_rbase, 1)
            dve.wait_ge(s_l0p, 2)
            for s in range(SEQS):
                norm0(2 * s)
                d.tensor_scalar(x_tok[:, (2 * s + 1) * P:(2 * s + 2) * P], acc[:, (2 * s + 1) * P:(2 * s + 2) * P],
                                mv0[:, 4 * s + 2:4 * s + 3], rs0[:, 2 * s + 1:2 * s + 2], ALU.subtract, ALU.mult)\
                 .then_inc(s_xready, 1)

            def first_attention(s):
                dve.wait_ge(s_xready, nth(1, s, 1))
                dve.wait_ge(s_a["t"], nth(1, s - 1, 1))
                d.tensor_copy(axin[:, :], x_tok[:, bass.ds(s * LEN, LEN)]).then_inc(s_a["xin"], 1)
                dve.wait_ge(s_a["qkv"], nth(3, s, 3))
                d.tensor_tensor(av[:, :].rearrange("p (t c) -> p t c", t=TILES),
                                pG[:, 0:LEN].rearrange("p (t c) -> p t c", t=TILES),
                                abv[:, :].unsqueeze(1).to_broadcast([P, TILES, P]), ALU.add).then_inc(s_a["v"], 1)
                dve.wait_ge(s_a["s"], nth(1, s, 1))
                d.tensor_reduce(am2[:, :], pS[:, :].rearrange("p (t k) -> p t k", t=TILES), op=ALU.max, axis=AX.X)\
                 .then_inc(s_a["max"], 1)
                dve.wait_ge(s_a["max"], nth(1, s, 1))
                d.tensor_scalar(am2[:, :], am2[:, :], -float(P) ** -0.5, None, ALU.mult).then_inc(s_a["neg"], 1)
                dve.wait_ge(s_a["exp"], nth(2, s, 2))
                d.reciprocal(ar2[:, :], as2[:, :]).then_inc(s_a["rec"], 1)
                dve.wait_ge(s_a["rec"], nth(1, s, 1))
                dve.wait_ge(s_a["o"], nth(1, s, 1))
                for T in range(TILES):
                    o = acc[:, bass.ds(s * LEN + T * P, P)]
                    last = d.scalar_tensor_tensor(out=o, in0=pO[:, T * P:(T + 1) * P], scalar=ar2[:, T:T + 1],
                                                  in1=o, op0=ALU.mult, op1=ALU.add)
                last.then_inc(s_a["done"], 1)

            first_attention(0)
            with dve.Fori(1, SEQS) as s:
                first_attention(s)

            def rotate(n, T, m):
                i, kind, b = 4 * T + m, 2 * (m // 2), (m % 2) * CH
                dve.wait_ge(s_sq, nth(8, n, i + 1))
                dve.wait_ge(s_add, nth(8, n, i - 1))
                src = heads(pQ[m % 2][:, :])
                d.tensor_tensor(heads(t1[:, b:b + CH]), src, table(n, kind, T), ALU.mult).then_inc(s_t1, 1)
                o2 = heads(t2[:, b:b + CH])
                d.tensor_tensor(o2[:, :, 0:HD], src[:, :, HD:], table(n, kind + 1, T, 0), ALU.mult)
                d.tensor_tensor(o2[:, :, HD:], src[:, :, 0:HD], table(n, kind + 1, T, 1), ALU.mult)\
                 .then_inc(s_rot, 1)
                d.tensor_reduce(n2[:, T * 2 * HEADS + m * CHH:T * 2 * HEADS + (m + 1) * CHH],
                                heads(sq[:, b:b + CH]), op=ALU.add, axis=AX.X).then_inc(s_n2, 1)
                if m % 2:
                    c = 2 * T + m // 2
                    w = slice(c * HEADS, (c + 1) * HEADS)
                    dve.wait_ge(s_n2, nth(8, n, i + 1))
                    dve.wait_ge(s_rn, nth(4, n - 1, c + 1))
                    d.tensor_scalar(n2c[:, w], n2[:, w], 1e-24, None, ALU.max).then_inc(s_n2c, 1)

            def scale_k(n, T, m):
                dve.wait_ge(s_add, nth(8, n, 4 * T + m + 1))
                dve.wait_ge(s_rn, nth(4, n, 2 * T + 2))
                c = heads(rot[:, (4 * T + m) * CH:(4 * T + m + 1) * CH])
                r = rnorm[:, T * 2 * HEADS + m * CHH:T * 2 * HEADS + (m + 1) * CHH]
                d.tensor_tensor(c, c, over(r, CHH, DH), ALU.mult).then_inc(s_ksc, 1)

            def less_max(n, u):
                dve.wait_ge(s_s, nth(4, n, u + 1))
                src = heads(pS[:, :])
                m = m8[:, (u % 2) * PAIRS:(u % 2 + 1) * PAIRS]
                d.tensor_reduce(m, src, op=ALU.max, axis=AX.X).then_inc(s_max, 1)
                dve.wait_ge(s_max, nth(4, n, u + 1))
                dve.wait_ge(s_pt, nth(4, n, u - 1))
                d.tensor_tensor(heads(es[:, (u % 2) * CH:(u % 2 + 1) * CH]), src, over(m, PAIRS, DH), ALU.subtract)\
                 .then_inc(s_sub, 1)

            def divide(n, u):
                dve.wait_ge(s_exp, nth(4, n, u + 1))
                e = heads(es[:, (u % 2) * CH:(u % 2 + 1) * CH])
                s_, r_ = (t[:, (u % 2) * PAIRS:(u % 2 + 1) * PAIRS] for t in (s8, r8))
                d.tensor_reduce(s_, e, op=ALU.add, axis=AX.X).then_inc(s_sum, 1)
                dve.wait_ge(s_sum, nth(4, n, u + 1))
                d.reciprocal(r_, s_).then_inc(s_rec, 1)
                dve.wait_ge(s_rec, nth(4, n, u + 1))
                d.tensor_tensor(e, e, over(r_, PAIRS, DH), ALU.mult).then_inc(s_p, 1)

            def middle(n, T):
                dve.wait_ge(s_wo, nth(2, n, T + 1))
                dve.wait_ge(s_f1, nth(1, n - 1, 1))
                dve.wait_ge(s_res, nth(1, n - 1, 1))
                d.tensor_tensor(xm[:, T * P:(T + 1) * P], pO[:, 0:P], tokens(x_tok, n, T), ALU.add)\
                 .then_inc(s_mid, 1)

            def stats(n):
                dve.wait_ge(s_f2, nth(1, n, 1))
                for T in range(TILES):
                    d.bn_stats(stat[:, T * 6:(T + 1) * 6], pF[:, T * P:(T + 1) * P]).then_inc(s_st, 1)
                dve.wait_ge(s_zero, 2)
                dve.wait_ge(s_st, nth(2, n, 2))
                for T in range(TILES):
                    d.bn_aggr(mv[:, T * 2:(T + 1) * 2], stat[:, T * 6:(T + 1) * 6]).then_inc(s_mv, 1)

            def normalise(n):
                dve.wait_ge(s_rstd, nth(1, n, 1))
                for T in range(TILES):
                    d.tensor_scalar(xn[:, T * P:(T + 1) * P], pF[:, T * P:(T + 1) * P], mv[:, 2 * T:2 * T + 1],
                                    rstd[:, T:T + 1], ALU.subtract, ALU.mult).then_inc(s_xn, 1)

            def affine(n):
                dve.wait_ge(s_f3, nth(1, n, 1))
                d.tensor_scalar(xg[:, :], pF[:, 0:LEN], gain[:, bass.ds(layer(n), 1)],
                                shift[:, bass.ds(layer(n), 1)], ALU.mult, ALU.add).then_inc(s_xg, 1)

            def bias_gate(n):
                dve.wait_ge(s_f4g, nth(1, n, 1))
                for T in range(TILES):
                    d.tensor_tensor(gt[:, T * HID:(T + 1) * HID], pH[T][:, 0:HID],
                                    b_1[:, bass.ds(par(n) * 2 * HID + HID, HID)], ALU.add).then_inc(s_gt, 1)

            def bias_hidden(n):
                dve.wait_ge(s_f4a, nth(1, n, 1))
                for T in range(TILES):
                    d.tensor_tensor(am[:, T * HID:(T + 1) * HID], pH[T][:, 0:HID],
                                    b_1[:, bass.ds(par(n) * 2 * HID, HID)], ALU.add).then_inc(s_am, 1)

            def gated(n):
                dve.wait_ge(s_gg, nth(1, n, 1))
                dve.wait_ge(s_am, nth(2, n, 2))
                d.tensor_tensor(am[:, :], am[:, :], gt[:, :], ALU.mult).then_inc(s_hm, 1)

            def finish(n):
                dve.wait_ge(s_f6, nth(1, n, 1))
                dve.wait_ge(s_res, nth(1, n, 1))
                for T in range(TILES):
                    o = tokens(x_tok, n, T)
                    last = d.tensor_tensor(o, pH[T][:, 0:P], o, ALU.add)
                last.then_inc(s_xready, 1)

            def iteration(n):
                nx, m = n + 1, n - 1
                if live(n):
                    rotate(n, 1, 3)
                if live(m - 1):
                    gated(m - 1)
                if live(n):
                    less_max(n, 0)
                if live(nx):
                    rotate(nx, 0, 0)
                if live(n):
                    divide(n, 0)
                if live(nx):
                    rotate(nx, 0, 1)
                if live(n):
                    scale_k(n, 1, 2)
                    less_max(n, 1)
                    scale_k(n, 1, 3)
                if live(m - 1):
                    finish(m - 1)
                if live(m):
                    middle(m, 1)
                if live(nx):
                    rotate(nx, 0, 2)
                if live(n):
                    divide(n, 1)
                if live(nx):
                    rotate(nx, 0, 3)
                if live(m):
                    stats(m)
                if live(n):
                    less_max(n, 2)
                if live(nx):
                    rotate(nx, 1, 0)
                if live(m):
                    normalise(m)
                if live(n):
                    divide(n, 2)
                if live(nx):
                    rotate(nx, 1, 1)
                    scale_k(nx, 0, 2)
                if live(n):
                    less_max(n, 3)
                if live(nx):
                    scale_k(nx, 0, 3)
                if live(m):
                    affine(m)
                if live(n):
                    middle(n, 0)
                if live(nx):
                    rotate(nx, 1, 2)
                if live(m):
                    bias_gate(m)
                if live(n):
                    divide(n, 3)
                if live(m):
                    bias_hidden(m)

            for n in range(-1, FIRST):
                iteration(n)
            with dve.Fori(FIRST, LAST) as n:
                iteration(n)
            for n in range(LAST, STEPS + 2):
                iteration(n)
            dve.wait_ge(s_xready, STEPS + SEQS)
            d.tensor_tensor(acc[:, :], acc[:, :], x_tok[:, :], ALU.add).then_inc(s_fin, 1)

        @block.tensor
        def _(pe):
            t = nc.tensor

            def mm(o, l, r, start=True, stop=True):
                return t.matmul(o, l, r, start=start, stop=stop, skip_group_check=True)

            pe.wait_ge(s_const, 16 * NCONST)
            pe.wait_ge(s_zero, 2)

            def first_attention(s):
                pe.wait_ge(s_a["xin"], nth(1, s, 1))
                for T in range(TILES):
                    last = t.transpose(pT[:, T * P:(T + 1) * P], axin[:, T * P:(T + 1) * P], ident[:, :])
                last.then_inc(s_a["t"], 1)
                pe.wait_ge(s_a["x"], nth(1, s, 1))
                mm(pQ[0][:, 0:LEN], aw[:, 0:P], ax[:, :]).then_inc(s_a["qkv"], 1)
                mm(pQ[1][:, 0:LEN], aw[:, P:2 * P], ax[:, :]).then_inc(s_a["qkv"], 1)
                for T in range(TILES):
                    last = mm(pG[:, T * P:(T + 1) * P], ax[:, T * P:(T + 1) * P], aw[:, 2 * P:3 * P])
                last.then_inc(s_a["qkv"], 1)
                pe.wait_ge(s_a["q"], nth(1, s, 1))
                pe.wait_ge(s_a["k"], nth(1, s, 1))
                for T in range(TILES):
                    last = mm(pS[:, T * LEN:(T + 1) * LEN], aq[:, T * P:(T + 1) * P], ak[:, :])
                last.then_inc(s_a["s"], 1)
                pe.wait_ge(s_a["exp"], nth(2, s, 2))
                for k in range(TILES):
                    for T in range(TILES):
                        last = t.transpose(pP[:, (k * TILES + T) * P:(k * TILES + T + 1) * P],
                                           ap_[:, T * LEN + k * P:T * LEN + (k + 1) * P], ident[:, :])
                last.then_inc(s_a["pt"], 1)
                pe.wait_ge(s_a["pte"], nth(1, s, 1))
                pe.wait_ge(s_a["v"], nth(1, s, 1))
                pe.wait_ge(s_a["done"], nth(1, s - 1, 1))
                for T in range(TILES):
                    for k in range(TILES):
                        last = mm(pO[:, T * P:(T + 1) * P], apt[:, (k * TILES + T) * P:(k * TILES + T + 1) * P],
                                  av[:, k * P:(k + 1) * P], start=k == 0, stop=k == TILES - 1)
                last.then_inc(s_a["o"], 1)

            first_attention(0)
            with pe.Fori(1, SEQS) as s:
                first_attention(s)
            pe.wait_ge(s_a["done"], SEQS)
            pe.wait_ge(s_w, 2 * 16 * WLOADS)

            def take_in(n):
                pe.wait_ge(s_xin, nth(1, n, 1))
                pe.wait_ge(s_qte, nth(12, n - 1, 6))
                for T in range(TILES):
                    last = t.transpose(pT[:, T * P:(T + 1) * P], xin[:, T * P:(T + 1) * P], ident[:, :])
                last.then_inc(s_xt, 1)

            def project(n, T, i):
                pe.wait_ge(s_xs, nth(4, n, 2 * T + 2))
                if i == 0 and T == 0:
                    pe.wait_ge(s_w, layer(n) * (16 * WLOADS) + 16 * WLOADS)
                if i >= 2:
                    pe.wait_ge(s_rot, nth(8, n, 4 * T + i - 1))
                elif T:
                    pe.wait_ge(s_v, nth(4, n, i + 1))
                else:
                    pe.wait_ge(s_v, nth(4, n - 1, 2 + i + 1))
                mm(pQ[i % 2][:, :], xs[:, T * P:(T + 1) * P], w_qkv[:, bass.ds(par(n) * QKV + i * CH, CH)])\
                    .then_inc(s_qkv, 1)

            def turn_qk(n, T, g):
                if g < 2:
                    pe.wait_ge(s_qsc, nth(4, n, 2 * T + g + 1))
                else:
                    pe.wait_ge(s_ksc, nth(4, n, 2 * T + g - 1))
                if g == 0 and T == 0:
                    pe.wait_ge(s_qte, nth(12, n - 1, 12))
                elif g == 0:
                    pe.wait_ge(s_qte, nth(12, n, 6))
                    if live(n + 1):
                        pe.wait_ge(s_xs, nth(4, n + 1, 4))
                else:
                    pe.wait_ge(s_qte, nth(12, n, 6 * T + (2 * g if g < 3 else 5)))
                for k in range(4):
                    last = t.transpose(pT[:, k * P:(k + 1) * P],
                                       rot[:, (4 * T + g) * CH + k * P:(4 * T + g) * CH + (k + 1) * P], ident[:, :])
                last.then_inc(s_qt, 1)

            def scores(n, u):
                T, al = u // 2, 1 - u % 2
                pe.wait_ge(s_qte, nth(12, n, 6 * T + 6))
                pe.wait_ge(s_sub, nth(4, n, u))
                first = int(T == 0 and al == 0)
                mm(pS[:, :], identh[:, :],
                   mask[:, first * 64:first * 64 + 64].unsqueeze(1).to_broadcast([P, PAIRS, 64]),
                   stop=False)
                for pair in range(PAIRS):
                    for s in range(2):
                        w = 4 * T + al + 2 * s
                        last = mm(pS[64 * s:64 * s + 64, pair * 64:pair * 64 + 64],
                                  qz[:, (pair * 8 + w) * 64:(pair * 8 + w) * 64 + 64],
                                  kt3[:, pair, WIN * w:WIN * w + 64], start=False, stop=pair == PAIRS - 1)
                last.then_inc(s_s, 1)

            def turn_p(n, u):
                pe.wait_ge(s_p, nth(4, n, u + 1))
                pe.wait_ge(s_pte, nth(16, n, 4 * u))
                for k in range(4):
                    c = (u % 2) * CH + k * P
                    last = t.transpose(pP[:, k * P:(k + 1) * P], es[:, c:c + P], ident[:, :])
                last.then_inc(s_pt, 1)

            def values(n, u):
                T, al = u // 2, 1 - u % 2
                pe.wait_ge(s_pte, nth(16, n, 4 * u + 4))
                if al:
                    pe.wait_ge(s_v, nth(4, n, 2 * T + 2))
                elif T:
                    pe.wait_ge(s_vb1, nth(32, n, 32))
                else:
                    pe.wait_ge(s_vb0, nth(16, n, 16))
                pe.wait_ge(s_ot, nth(4, n, u))
                if al:
                    pe.wait_ge(s_mid, nth(2, n, T))
                src = v if al else vb
                for h in range(HEADS):
                    pair, hh = h // 2, h % 2
                    last = mm(pO[64 * hh:64 * hh + 64, pair * 64:pair * 64 + 64],
                              src[:, T * INNER + h * DH:T * INNER + (h + 1) * DH],
                              pz5[:, u % 2, pair, :, hh, :])
                last.then_inc(s_av, 1)

            def project_out(n, T):
                pe.wait_ge(s_ot, nth(4, n, 2 * T + 2))
                for pair in range(PAIRS):
                    last = mm(pO[:, 0:P], ot[:, pair * LEN + T * P:pair * LEN + (T + 1) * P],
                              w_o[:, bass.ds(par(n) * (PAIRS * P) + pair * P, P)],
                              start=pair == 0, stop=pair == PAIRS - 1)
                last.then_inc(s_wo, 1)

            def turn_to_pF(src, signal):
                for T in range(TILES):
                    last = t.transpose(pF[:, T * P:(T + 1) * P], src[:, T * P:(T + 1) * P], ident[:, :])
                last.then_inc(signal, 1)

            def hidden(n, half):
                if half:
                    pe.wait_ge(s_xg, nth(1, n, 1))
                else:
                    pe.wait_ge(s_gt, nth(2, n, 2))
                for T in range(TILES):
                    last = mm(pH[T][:, 0:HID], xg[:, T * P:(T + 1) * P],
                              w_1[:, bass.ds(par(n) * 2 * HID + half * HID, HID)])
                last.then_inc(s_f4g if half else s_f4a, 1)

            def turn_h(n):
                pe.wait_ge(s_hm, nth(1, n, 1))
                for T in range(TILES):
                    for j in range(HCH):
                        w = P if j < 2 else HLAST
                        c = T * HID + j * P
                        last = t.transpose(pH[T][0:w, j * P:(j + 1) * P], am[:, c:c + w], ident[:, :])
                last.then_inc(s_f5, 1)

            def down(n):
                pe.wait_ge(s_ht, nth(4, n, 4))
                for T in range(TILES):
                    for j in range(HCH):
                        k = P if j < 2 else HLAST + 1
                        c = (T * HCH + j) * P
                        last = mm(pH[T][:, 0:P], ht[0:k, c:c + P],
                                  w_2[0:k, bass.ds(par(n) * (HCH * P) + j * P, P)], start=j == 0, stop=j == HCH - 1)
                last.then_inc(s_f6, 1)

            def iteration(n):
                nx, m = n + 1, n - 1
                if live(m):
                    turn_p(m, 3)
                if live(nx):
                    take_in(nx)
                if live(n):
                    project(n, 1, 4)
                    scores(n, 0)
                    project(n, 1, 5)
                if live(m - 1):
                    turn_h(m - 1)
                if live(nx):
                    project(nx, 0, 0)
                if live(m):
                    values(m, 3)
                if live(nx):
                    project(nx, 0, 1)
                if live(m - 1):
                    down(m - 1)
                if live(n):
                    turn_p(n, 0)
                    turn_qk(n, 1, 0)
                    scores(n, 1)
                    turn_qk(n, 1, 1)
                if live(nx):
                    project(nx, 0, 2)
                if live(m):
                    project_out(m, 1)
                if live(n):
                    values(n, 0)
                if live(m):
                    pe.wait_ge(s_mid, nth(2, m, 2))
                    pe.wait_ge(s_xready, nth(1, m - 1, SEQS + 1))
                    turn_to_pF(xm, s_f1)
                if live(n):
                    turn_qk(n, 1, 2)
                if live(nx):
                    project(nx, 0, 3)
                if live(m):
                    pe.wait_ge(s_xf, nth(2, m, 2))
                    turn_to_pF(xf, s_f2)
                if live(n):
                    turn_qk(n, 1, 3)
                    turn_p(n, 1)
                    scores(n, 2)
                if live(nx):
                    project(nx, 0, 4)
                    project(nx, 0, 5)
                    project(nx, 1, 0)
                if live(n):
                    values(n, 1)
                if live(nx):
                    project(nx, 1, 1)
                if live(m):
                    pe.wait_ge(s_xn, nth(2, m, 2))
                    turn_to_pF(xn, s_f3)
                if live(n):
                    turn_p(n, 2)
                    scores(n, 3)
                if live(nx):
                    turn_qk(nx, 0, 0)
                    project(nx, 1, 2)
                    turn_qk(nx, 0, 1)
                if live(n):
                    project_out(n, 0)
                if live(m):
                    hidden(m, 1)
                if live(n):
                    values(n, 2)
                if live(nx):
                    turn_qk(nx, 0, 2)
                    project(nx, 1, 3)
                if live(m):
                    hidden(m, 0)
                if live(nx):
                    turn_qk(nx, 0, 3)

            for n in range(-1, FIRST):
                iteration(n)
            with pe.Fori(FIRST, LAST) as n:
                iteration(n)
            for n in range(LAST, STEPS + 2):
                iteration(n)


def constants():
    f = np.float32
    half = np.arange(0, DH, 2, dtype=f)
    inv_freq = (f(1.0) / np.power(f(10000.0), half / f(DH))).astype(f)
    t = np.arange(LEN, dtype=f)
    freqs = (t[:, None] * inv_freq[None, :]).astype(f)
    base = ((half + f(0.4 * DH)) / f(1.4 * DH)).astype(f)
    power = (t - f(LEN // 2)) / f(WIN // 2)
    scale = np.power(base[None, :], power[:, None]).astype(f)
    cos, sin = np.cos(freqs), np.sin(freqs)
    rows = []
    for s in (scale, f(1.0) / scale):
        rows.append(np.concatenate([cos * s, cos * s], 1))
        rows.append(np.concatenate([-sin * s, sin * s], 1))
    rot_base = np.stack(rows).reshape(4, TILES, P, DH).transpose(2, 0, 1, 3).reshape(P, -1).astype(f)
    q = np.arange(P) % WIN
    j = np.arange(2 * WIN)
    seen = np.where(j[None, :] < WIN, q[:, None] <= j[None, :], j[None, :] - WIN <= q[:, None])
    first = seen & ((np.arange(P)[:, None] >= 64) | (j[None, :] >= WIN))
    masks = np.where(np.concatenate([seen, first], 1), 0.0, MASKED).astype(f)
    return {"rot_base": rot_base, "masks": masks, "ident_f": np.eye(P, dtype=f)}


_INS = ["X", "W_q", "W_k", "W_v", "b_q", "b_k", "b_v"]
_FFN = ["Wqkv", "q_scale", "k_scale", "Wo", "ln_g", "ln_b", "W1", "b1", "W2", "b2"]
_FLAT = {"Wqkv": (DEPTH * P, QKV), "Wo": (DEPTH * INNER, P), "W1": (DEPTH * P, 2 * HID), "W2": (DEPTH * HID, P)}


def kernel(**inputs):
    import concourse.bacc as _bacc
    from concourse.bass_utils import run_bass_kernel_spmd as _run

    nc = _bacc.Bacc("TRN2", target_bir_lowering=False, num_devices=1)
    arrays = {}
    for n in _INS:
        arrays[n] = np.ascontiguousarray(inputs["L0_attn_" + n])
    for n in _FFN:
        a = np.ascontiguousarray(inputs["L0_ffn_" + n])
        arrays[n] = a.reshape(_FLAT[n]) if n in _FLAT else a
    arrays.update(constants())
    arrays = {f"in_{n}": a for n, a in arrays.items()}
    args = [nc.dram_tensor(n, a.shape, mybir.dt.from_np(a.dtype), kind="ExternalInput").ap()
            for n, a in arrays.items()]
    out = nc.dram_tensor("out", (SEQS, LEN, P), F32, kind="ExternalOutput").ap()
    program(nc, *args, out)
    r = _run(nc, [arrays], core_ids=[0])
    return r.results[0]["out"]
```

```python
from contextlib import ExitStack

import concourse.bass as bass
import numpy as np
from concourse import mybir

F32 = mybir.dt.float32
F32R = mybir.dt.float32r
BF16 = mybir.dt.bfloat16
ALU = mybir.AluOpType
ACT = mybir.ActivationFunctionType
AX = mybir.AxisListType

P = 128
SEQS, LEN = 8, 256
TILES = LEN // P
DEPTH, HEADS, DH, WIN = 6, 16, 64, 32
INNER = HEADS * DH
HD = DH // 2
PAIRS = HEADS // 2
HID = int(P * 4 * 2 / 3)
HCH = 3
HLAST = HID - 2 * P
STEPS = DEPTH * SEQS
CH = 512
CHH = CH // DH
QKV = 3 * INNER
WLOADS = 7
WCH = QKV // CH
MASKED = -1.0e30
FIRST, LAST = 2, STEPS - 2
EPS = 1e-5


def nth(per, n, e):
    value = n * per + e
    if isinstance(value, int):
        return max(0, value)
    assert value.min_val > 0
    return value


def live(n):
    return not isinstance(n, int) or 0 <= n < STEPS


def program(nc, X, Wq, Wk, Wv, bq, bk, bv, Wqkv, q_scale, k_scale, Wo, ln_g, ln_b, W1, b1, W2, b2,
            rot_base, masks, ident_f, out):
    ctx = ExitStack()
    with ctx:
        def sb(name, cols, dt=F32):
            return ctx.enter_context(nc.sbuf_tensor(name, [P, cols], dt))

        def sem(name):
            return ctx.enter_context(nc.semaphore(name))

        ident = sb("ident", P)
        identh = sb("identh", P, BF16)
        mask = sb("mask", 2 * 64, BF16)
        maskf = sb("maskf", 2 * 64)
        x_tok = sb("x_tok", SEQS * TILES * P)
        acc = sb("acc", SEQS * TILES * P)
        w_new = sb("w_new", QKV)
        w_hi = sb("w_hi", QKV, F32R)
        w_lo = sb("w_lo", QKV, F32R)
        w_o = sb("w_o", 2 * PAIRS * P)
        w_1 = sb("w_1", 2 * 2 * HID)
        w_2 = sb("w_2", 2 * HCH * P)
        b_1 = sb("b_1", 2 * 2 * HID)
        gain = sb("gain", DEPTH)
        shift = sb("shift", DEPTH)
        rbase = sb("rbase", 4 * TILES * DH)
        scales = sb("scales", 2 * DEPTH * DH)
        rtab = sb("rtab", DEPTH * 4 * TILES * DH)
        xin = sb("xin", TILES * P)
        x_hi = sb("x_hi", LEN, F32R)
        x_lo = sb("x_lo", LEN, F32R)
        sq = sb("sq", 2 * CH)
        t1 = sb("t1", 2 * CH)
        t2 = sb("t2", 2 * CH)
        rot = sb("rot", TILES * 4 * CH)
        n2 = sb("n2", TILES * 2 * HEADS)
        n2c = sb("n2c", TILES * 2 * HEADS)
        rnorm = sb("rnorm", TILES * 2 * HEADS)
        minus_half = sb("minus_half", HEADS)
        eps = sb("eps", TILES)
        qz = sb("qz", PAIRS * 8 * 64)
        kt = sb("kt", PAIRS * (WIN + LEN))
        v = sb("v", TILES * INNER)
        vb = sb("vb", TILES * INNER)
        es = sb("es", 2 * CH)
        m8 = sb("m8", 2 * PAIRS)
        s8 = sb("s8", 2 * PAIRS)
        r8 = sb("r8", 2 * PAIRS)
        pz = sb("pz", 2 * PAIRS * P)
        ot = sb("ot", PAIRS * LEN)
        xm = sb("xm", TILES * P)
        xf = sb("xf", LEN)
        stat = sb("stat", TILES * 6)
        mv = sb("mv", TILES * 2)
        ve = sb("ve", TILES)
        rstd = sb("rstd", TILES)
        xn = sb("xn", TILES * P)
        xg = sb("xg", LEN)
        gt = sb("gt", TILES * HID)
        am = sb("am", TILES * HID)
        ht = sb("ht", TILES * HCH * P)
        place = 0

        def early(cols):
            nonlocal place
            place += cols
            return rot[:, place - cols:place]

        aw = early(3 * P)
        abv = early(P)
        axin = early(LEN)
        ax = early(LEN)
        aq = early(LEN)
        ak = early(LEN)
        av = early(2 * LEN)
        aprob = early(TILES * LEN)
        apt = early(TILES * LEN)
        abq = sb("abq", 2)
        st0 = sb("st0", SEQS * TILES * 6)
        mv0 = sb("mv0", SEQS * TILES * 2)
        ve0 = sb("ve0", SEQS * TILES)
        rs0 = sb("rs0", SEQS * TILES)
        am2 = sb("am2", TILES)
        as2 = sb("as2", TILES)
        ar2 = sb("ar2", TILES)

        bank = [ctx.enter_context(nc.psum_tensor(f"bank{i}", [P, CH], F32)) for i in range(8)]
        pQ = bank[0:2]
        pT, pS, pP, pO, pF, pG = bank[2:8]
        pH = (pG, pF)
        pV = (pG, pG, pS, pO)

        s_const = sem("s_const")
        s_x = sem("s_x")
        s_wq = sem("s_wq")
        s_wh = sem("s_wh")
        s_wl = sem("s_wl")
        s_w = sem("s_w")
        s_zero = sem("s_zero")
        s_rbase = sem("s_rbase")
        s_xready = sem("s_xready")
        s_xin = sem("s_xin")
        s_xt = sem("s_xt")
        s_xs = sem("s_xs")
        s_xl = sem("s_xl")
        s_qk = sem("s_qk")
        s_vp = sem("s_vp")
        s_sq = sem("s_sq")
        s_t1 = sem("s_t1")
        s_rot = sem("s_rot")
        s_n2 = sem("s_n2")
        s_add = sem("s_add")
        s_n2c = sem("s_n2c")
        s_rn = sem("s_rn")
        s_qsc = sem("s_qsc")
        s_ksc = sem("s_ksc")
        s_qt = sem("s_qt")
        s_qte = sem("s_qte")
        s_v = sem("s_v")
        s_vb0 = sem("s_vb0")
        s_vb1 = sem("s_vb1")
        s_s = sem("s_s")
        s_max = sem("s_max")
        s_sub = sem("s_sub")
        s_exp = sem("s_exp")
        s_sum = sem("s_sum")
        s_rec = sem("s_rec")
        s_p = sem("s_p")
        s_pt = sem("s_pt")
        s_pte = sem("s_pte")
        s_av = sem("s_av")
        s_ot = sem("s_ot")
        s_wo = sem("s_wo")
        s_mid = sem("s_mid")
        s_res = sem("s_res")
        s_f1 = sem("s_f1")
        s_xf = sem("s_xf")
        s_f2 = sem("s_f2")
        s_st = sem("s_st")
        s_mv = sem("s_mv")
        s_ve = sem("s_ve")
        s_rstd = sem("s_rstd")
        s_xn = sem("s_xn")
        s_f3 = sem("s_f3")
        s_xg = sem("s_xg")
        s_f4g = sem("s_f4g")
        s_gt = sem("s_gt")
        s_gg = sem("s_gg")
        s_f4a = sem("s_f4a")
        s_am = sem("s_am")
        s_hm = sem("s_hm")
        s_f5 = sem("s_f5")
        s_ht = sem("s_ht")
        s_f6 = sem("s_f6")
        s_l0 = sem("s_l0")
        s_l0p = sem("s_l0p")
        s_a = {k: sem("s_a_" + k) for k in ("xin", "t", "x", "qkv", "q", "k", "v", "s", "max", "neg", "exp",
                                            "rec", "pt", "pte", "o", "done")}
        s_fin = sem("s_fin")
        s_out = sem("s_out")

        def layer(n):
            return n // SEQS

        def par(n):
            return (n // SEQS) % 2

        def tokens(t, n, T, k=1):
            return t[:, bass.ds((n % SEQS) * (TILES * P) + T * P, k * P)]

        def heads(a):
            return a.rearrange("p (h c) -> p h c", c=DH)

        def table(n, kind, T, half=None):
            off = layer(n) * (4 * TILES * DH) + (kind * TILES + T) * DH
            w = DH
            if half is not None:
                off, w = off + half * (DH // 2), DH // 2
            return rtab[:, bass.ds(off, w)].unsqueeze(1).to_broadcast([P, CHH, w])

        def over(a, k, w):
            return a.unsqueeze(2).to_broadcast([P, k, w])

        qz5 = qz[:, :].rearrange("p (a w h q) -> p a w h q", a=PAIRS, w=8, h=2)
        kt3 = kt[:, :].rearrange("p (a t) -> p a t", a=PAIRS)
        pz4 = pz[:, :].rearrange("p (b a s c) -> p b a s c", b=2, a=PAIRS, s=2)
        pz5 = pz[:, :].rearrange("p (b a s h q) -> p b a s h q", b=2, a=PAIRS, s=2, h=2)
        ot6 = ot[:, :].rearrange("p (a t s l q) -> p a t s l q", a=PAIRS, t=TILES, s=2, l=2)

        def some(s):
            return not isinstance(s, int) or 0 <= s < SEQS

        block = ctx.enter_context(nc.Block())

        def chunk_of(i):
            return i * CH, (i if i < 4 else None)

        @block.sync
        def _(sp):
            sp.dma_start(acc[:, :].rearrange("p (s t c) -> p s t c", s=SEQS, t=TILES),
                         X.rearrange("s (t p) c -> p s t c", p=P)).then_inc(s_x, 16)
            for dst, src in ((ident[:, :], ident_f), (maskf[:, :], masks),
                             (rbase[:, :], rot_base),
                             (aw[:, 0:P], Wq), (aw[:, P:2 * P], Wk), (aw[:, 2 * P:3 * P], Wv),
                             (abq[:, 0:1], bq.rearrange("(p a) -> p a", a=1)),
                             (abq[:, 1:2], bk.rearrange("(p a) -> p a", a=1)),
                             (abv[:, :], bv.partition_broadcast(P)),
                             (scales[:, 0:DEPTH * DH], q_scale.rearrange("l c -> (l c)").partition_broadcast(P)),
                             (scales[:, DEPTH * DH:], k_scale.rearrange("l c -> (l c)").partition_broadcast(P)),
                             ):
                sp.dma_start(dst, src).then_inc(s_const, 16)
            for dst, src in ((gain, ln_g), (shift, ln_b)):
                sp.dma_start(dst[:, :], src.rearrange("l c -> c l"), allow_slow_non_contiguous=True)\
                  .then_inc(s_const, 16)

            def weights(l):
                p = l % 2
                sp.dma_start(w_o[:, bass.ds(p * PAIRS * P, PAIRS * P)].rearrange("p (a c) -> p a c", a=PAIRS),
                             Wo[bass.ds(l * INNER, INNER), :].rearrange("(a p) c -> p a c", p=P)).then_inc(s_w, 16)
                sp.dma_start(w_1[:, bass.ds(p * 2 * HID, 2 * HID)], W1[bass.ds(l * P, P), :]).then_inc(s_w, 16)
                for j in range(HCH):
                    rows = P if j < 2 else HLAST
                    sp.dma_start(w_2[0:rows, bass.ds(p * HCH * P + j * P, P)],
                                 W2[bass.ds(l * HID + j * P, rows), :]).then_inc(s_w, 16)
                sp.dma_start(w_2[HLAST:HLAST + 1, bass.ds(p * HCH * P + 2 * P, P)], b2[bass.ds(l, 1), :])\
                  .then_inc(s_w, 16)
                sp.dma_start(b_1[:, bass.ds(p * 2 * HID, 2 * HID)],
                             b1[bass.ds(l, 1), :].to_broadcast([P, 2 * HID])).then_inc(s_w, 16)

            def qkv_weights(l):
                sp.wait_ge(s_wl, nth(WCH, l - 1, WCH))
                sp.dma_start(w_new[:, :], Wqkv[l * P:(l + 1) * P, :]).then_inc(s_wq, 16)

            qkv_weights(0)
            weights(0)
            weights(1)
            qkv_weights(1)

            def copy_v(n):
                sp.wait_ge(s_v, nth(4, n, 3))
                sp.dma_start(vb[WIN:P, 0:INNER], v[0:P - WIN, 0:INNER]).then_inc(s_vb0, 16)
                sp.wait_ge(s_ot, nth(4, n, 0))
                if isinstance(n, int) and n == 0:
                    sp.wait_ge(s_v, 4)
                sp.dma_start(vb[0:WIN, INNER:], v[P - WIN:P, 0:INNER]).then_inc(s_vb1, 16)
                sp.dma_start(vb[WIN:P, INNER:], v[0:P - WIN, INNER:]).then_inc(s_vb1, 16)

            sp.wait_ge(s_zero, 2)
            copy_v(0)
            with sp.Fori(1, SEQS) as n:
                copy_v(n)
            for l in range(1, DEPTH):
                for n in range(l * SEQS, l * SEQS + 3):
                    copy_v(n)
                if l < DEPTH - 1:
                    sp.wait_ge(s_xready, l * SEQS + SEQS)
                    weights(l + 1)
                    qkv_weights(l + 1)
                with sp.Fori(l * SEQS + 3, (l + 1) * SEQS) as n:
                    copy_v(n)
            sp.wait_ge(s_fin, 1)
            sp.dma_start(out.rearrange("s (t p) c -> p s t c", p=P),
                         acc[:, :].rearrange("p (s t c) -> p s t c", s=SEQS, t=TILES)).then_inc(s_out, 16)
            sp.wait_ge(s_out, 16)

        NCONST = 13

        @block.gpsimd
        def _(pool):
            g = nc.gpsimd
            g.memset(minus_half[:, :], -0.5)
            g.memset(eps[:, :], EPS)
            g.memset(qz[:, :], 0.0)
            g.memset(kt[:, :], 0.0)
            g.memset(xf[:, :], 0.0).then_inc(s_zero, 1)

            pool.wait_ge(s_l0, 2 * SEQS * TILES)
            g.tensor_scalar(ve0[:, :].unsqueeze(2), mv0[:, :].rearrange("p (k a) -> p k a", a=2)[:, :, 1:2],
                            EPS, 1.0, ALU.add, ALU.mult).then_inc(s_l0p, 1)
            pool.wait_ge(s_l0p, 1)
            g.tensor_tensor(rs0[:, :], ve0[:, :], minus_half[:, 0:SEQS * TILES], ALU.pow).then_inc(s_l0p, 1)

            pool.wait_ge(s_const, 16 * NCONST)
            rt = rtab[:, :].rearrange("p (l k t c) -> p l k t c", l=DEPTH, k=4, t=TILES)
            rb = rbase[:, :].rearrange("p (k t c) -> p k t c", k=4, t=TILES)
            sc = scales[:, :].rearrange("p (z l c) -> p z l c", z=2, l=DEPTH)
            for z in range(2):
                for T in range(TILES):
                    g.tensor_tensor(rt[:, :, 2 * z, T, :], sc[:, z],
                                    rb[:, 2 * z, T, :].unsqueeze(1).to_broadcast([P, DEPTH, DH]), ALU.mult)
                    for h in range(2):
                        last = g.tensor_tensor(
                            rt[:, :, 2 * z + 1, T, h * HD:(h + 1) * HD], sc[:, z, :, (1 - h) * HD:(2 - h) * HD],
                            rb[:, 2 * z + 1, T, h * HD:(h + 1) * HD].unsqueeze(1).to_broadcast([P, DEPTH, HD]),
                            ALU.mult)
            last.then_inc(s_rbase, 1)

            def add(n, T, m):
                i = 4 * T + m
                pool.wait_ge(s_rot, nth(8, n, i + 1))
                pool.wait_ge(s_qt, nth(8, n - 1, 4 * T + 4))
                b = (m % 2) * CH
                g.tensor_tensor(rot[:, i * CH:(i + 1) * CH], t1[:, b:b + CH], t2[:, b:b + CH], ALU.add)\
                 .then_inc(s_add, 1)

            def norms(n, T, k):
                w = slice((2 * T + k) * HEADS, (2 * T + k + 1) * HEADS)
                pool.wait_ge(s_n2c, nth(4, n, 2 * T + k + 1))
                if k:
                    pool.wait_ge(s_ksc, nth(4, n - 1, 2 * T + 2))
                g.tensor_tensor(rnorm[:, w], n2c[:, w], minus_half[:, :], ALU.pow).then_inc(s_rn, 1)

            def scale_q(n, T, m):
                pool.wait_ge(s_add, nth(8, n, 4 * T + m + 1))
                pool.wait_ge(s_rn, nth(4, n, 2 * T + 1))
                c = heads(rot[:, (4 * T + m) * CH:(4 * T + m + 1) * CH])
                r = rnorm[:, T * 2 * HEADS + m * CHH:T * 2 * HEADS + (m + 1) * CHH]
                g.tensor_tensor(c, c, over(r, CHH, DH), ALU.mult).then_inc(s_qsc, 1)

            def divide(n, u):
                pool.wait_ge(s_rec, nth(4, n, u + 1))
                e = heads(es[:, (u % 2) * CH:(u % 2 + 1) * CH])
                g.tensor_tensor(e, e, over(r8[:, (u % 2) * PAIRS:(u % 2 + 1) * PAIRS], PAIRS, DH), ALU.mult)\
                 .then_inc(s_p, 1)

            def rstd_(n):
                pool.wait_ge(s_mv, nth(2, n, 2))
                g.tensor_tensor(ve[:, :].unsqueeze(2), mv[:, :].rearrange("p (k a) -> p k a", a=2)[:, :, 1:2],
                                eps[:, :].unsqueeze(2), ALU.add).then_inc(s_ve, 1)
                pool.wait_ge(s_ve, nth(1, n, 1))
                g.tensor_tensor(rstd[:, :], ve[:, :], minus_half[:, 0:TILES], ALU.pow).then_inc(s_rstd, 1)

            def iteration(n):
                nx, m = n + 1, n - 1
                if live(n):
                    scale_q(n, 0, 1)
                if live(m):
                    divide(m, 2)
                if live(m - 1):
                    rstd_(m - 1)
                if live(n):
                    add(n, 1, 0)
                    add(n, 1, 1)
                    norms(n, 1, 0)
                if live(m):
                    divide(m, 3)
                if live(n):
                    add(n, 1, 2)
                    scale_q(n, 1, 0)
                    add(n, 1, 3)
                    scale_q(n, 1, 1)
                    norms(n, 1, 1)
                if live(nx):
                    add(nx, 0, 0)
                    add(nx, 0, 1)
                    norms(nx, 0, 0)
                if live(n):
                    divide(n, 0)
                if live(nx):
                    scale_q(nx, 0, 0)
                if live(n):
                    divide(n, 1)
                if live(nx):
                    add(nx, 0, 2)
                    add(nx, 0, 3)
                    norms(nx, 0, 1)

            for n in range(-2, FIRST):
                iteration(n)
            with pool.Fori(FIRST, LAST) as n:
                iteration(n)
            for n in range(LAST, STEPS + 2):
                iteration(n)

        @block.scalar
        def _(act):
            a = nc.scalar
            act.wait_ge(s_const, 16 * NCONST)
            act.wait_ge(s_zero, 2)

            def first_copy_p(s):
                act.wait_ge(s_a["pt"], nth(1, s, 1))
                act.wait_ge(s_a["o"], nth(1, s - 1, 1))
                a.activation(apt[:, :], pP[:, :], ACT.Copy).then_inc(s_a["pte"], 1)

            def first_copy_x(s):
                act.wait_ge(s_a["t"], nth(1, s, 1))
                act.wait_ge(s_a["qkv"], nth(3, s - 1, 3))
                a.activation(ax[:, :], pT[:, 0:LEN], ACT.Copy).then_inc(s_a["x"], 1)

            def first_bias(s):
                act.wait_ge(s_a["qkv"], nth(3, s, 1))
                act.wait_ge(s_a["s"], nth(1, s - 1, 1))
                a.activation(aq[:, :], pQ[0][:, 0:LEN], ACT.Identity, bias=abq[:, 0:1]).then_inc(s_a["q"], 1)
                act.wait_ge(s_a["qkv"], nth(3, s, 2))
                a.activation(ak[:, :], pQ[1][:, 0:LEN], ACT.Identity, bias=abq[:, 1:2]).then_inc(s_a["k"], 1)

            def first_exps(s):
                act.wait_ge(s_a["neg"], nth(1, s, 1))
                act.wait_ge(s_a["pt"], nth(1, s - 1, 1))
                act.wait_ge(s_a["rec"], nth(1, s - 1, 1))
                for T in range(TILES):
                    a.activation(aprob[:, T * LEN:(T + 1) * LEN], pS[:, T * LEN:(T + 1) * LEN], ACT.Exp,
                                 scale=float(P) ** -0.5, bias=am2[:, T:T + 1],
                                 accum_out=as2[:, T:T + 1]).then_inc(s_a["exp"], 1)

            def first_attention(s):
                if some(s - 1):
                    first_copy_p(s - 1)
                if some(s + 1):
                    first_copy_x(s + 1)
                if some(s):
                    first_exps(s)
                if some(s + 1):
                    first_bias(s + 1)

            for s in (-1, 0, 1):
                first_attention(s)
            with act.Fori(2, SEQS - 1) as s:
                first_attention(s)
            for s in (SEQS - 1, SEQS):
                first_attention(s)

            def copy_in(n):
                act.wait_ge(s_xready, nth(1, n, 1))
                act.wait_ge(s_xt, nth(1, n - 1, 1))
                a.activation(xin[:, :], tokens(x_tok, n, 0, TILES), ACT.Copy).then_inc(s_xin, 1)

            def residual(n):
                act.wait_ge(s_mid, nth(2, n, 2))
                a.activation(tokens(x_tok, n, 0, TILES), xm[:, :], ACT.Copy).then_inc(s_res, 1)

            def split_hi(n, chunks):
                def body():
                    act.wait_ge(s_wq, layer(n) * 16 + 16)
                    if chunks[-1] < 4:
                        act.wait_ge(s_qk, nth(8, n - 1, 4 + chunks[-1] + 1))
                    else:
                        act.wait_ge(s_vp, nth(4, n - 1, 4))
                    for c in chunks:
                        a.activation(w_hi[:, c * CH:(c + 1) * CH], w_new[:, c * CH:(c + 1) * CH], ACT.Copy)\
                         .then_inc(s_wh, 1)

                if not isinstance(n, int):
                    with act.If(n % SEQS == 0):
                        body()
                elif n % SEQS == 0 and live(n):
                    body()

            def shifted(n, T):
                act.wait_ge(s_xt, nth(1, n, 1))
                act.wait_ge(s_vp, nth(4, n - 1, 2 * T + 2))
                a.activation(x_hi[0:64, T * P:(T + 1) * P], pT[0:64, T * P:(T + 1) * P], ACT.Copy).then_inc(s_xs, 1)
                lo = max(1, T * P)
                a.activation(x_hi[64:P, lo:(T + 1) * P], pT[64:P, lo - 1:(T + 1) * P - 1], ACT.Copy)\
                 .then_inc(s_xs, 1)

            def square(n, T, m):
                i = 4 * T + m
                act.wait_ge(s_qk, nth(8, n, i + 1))
                act.wait_ge(s_n2, nth(8, n, i - 1))
                a.activation(sq[:, (m % 2) * CH:(m % 2 + 1) * CH], pQ[m % 2][:, :], ACT.Square).then_inc(s_sq, 1)

            def copy_v(n, T, c):
                act.wait_ge(s_vp, nth(4, n, 2 * T + c + 1))
                act.wait_ge(s_av, nth(4, n - 1, 2 * T + 1))
                act.wait_ge(s_vb1, nth(32, n - 1, 32))
                if T == 0:
                    act.wait_ge(s_vb0, nth(16, n - 1, 16))
                a.activation(v[:, T * INNER + c * CH:T * INNER + (c + 1) * CH], pV[2 * T + c][:, :], ACT.Copy)\
                 .then_inc(s_v, 1)

            def take_qk(n, T, g):
                act.wait_ge(s_qt, nth(8, n, 4 * T + g + 1))
                act.wait_ge(s_s, nth(4, n - 1, 2 if T == 0 and g < 2 else 4))
                pr = slice(4 * (g % 2), 4 * (g % 2) + 4)
                src = pT[:, :].rearrange("p (a w q) -> p a w q", a=4, w=4)
                if g < 2:
                    for h in range(2):
                        r = slice(64 * h, 64 * h + 64)
                        a.activation(qz5[r, pr, 4 * T:4 * T + 4, h, :], src[r], ACT.Copy).then_inc(s_qte, 1)
                else:
                    a.activation(kt3[:, pr, WIN + T * P:WIN + (T + 1) * P],
                                 pT[:, :].rearrange("p (a t) -> p a t", a=4), ACT.Copy).then_inc(s_qte, 1)

            def exps(n, u):
                act.wait_ge(s_sub, nth(4, n, u + 1))
                e = es[:, (u % 2) * CH:(u % 2 + 1) * CH]
                a.activation(e, e, ACT.Exp, scale=8.0).then_inc(s_exp, 1)

            def take_p(n, u):
                act.wait_ge(s_pt, nth(4, n, u + 1))
                act.wait_ge(s_av, nth(4, n, u - 1))
                src = pP[:, :].rearrange("p (a s c) -> p a s c", a=4, s=2)
                for odd in range(2):
                    for s in range(2):
                        a.activation(pz4[64 * s:64 * s + 64, u % 2, odd::2, s, :],
                                     src[64 * odd:64 * odd + 64, :, s, :], ACT.Copy).then_inc(s_pte, 1)

            def take_o(n, u):
                T, al = u // 2, 1 - u % 2
                act.wait_ge(s_av, nth(4, n, u + 1))
                act.wait_ge(s_wo, nth(2, n - 1, T + 1))
                a.activation(ot6[:, :, T, :, al, :], pO[:, :].rearrange("p (a s q) -> p a s q", a=PAIRS, s=2),
                             ACT.Copy).then_inc(s_ot, 1)

            def shifted_f(n):
                act.wait_ge(s_f1, nth(1, n, 1))
                a.activation(xf[0:64, :], pF[0:64, 0:LEN], ACT.Copy).then_inc(s_xf, 1)
                a.activation(xf[64:P, 1:LEN], pF[64:P, 0:LEN - 1], ACT.Copy).then_inc(s_xf, 1)

            def affine(n):
                act.wait_ge(s_f3, nth(1, n, 1))
                a.activation(xg[:, :], pF[:, 0:LEN], ACT.Identity, bias=shift[:, bass.ds(layer(n), 1)],
                             scale=gain[:, bass.ds(layer(n), 1)]).then_inc(s_xg, 1)

            def gelu(n):
                act.wait_ge(s_gt, nth(2, n, 2))
                a.activation(gt[:, :], gt[:, :], ACT.Gelu).then_inc(s_gg, 1)

            def take_h(n):
                act.wait_ge(s_f5, nth(1, n, 1))
                for T in range(TILES):
                    o = T * HCH * P
                    a.activation(ht[:, o:o + 2 * P], pH[T][:, 0:2 * P], ACT.Copy).then_inc(s_ht, 1)
                    a.activation(ht[0:HLAST, o + 2 * P:o + 3 * P], pH[T][0:HLAST, 2 * P:3 * P], ACT.Copy)\
                     .then_inc(s_ht, 1)

            def iteration(n):
                nx, m = n + 1, n - 1
                if live(m):
                    take_o(m, 1)
                if live(n):
                    square(n, 1, 1)
                if live(m):
                    exps(m, 3)
                if live(n):
                    take_qk(n, 0, 1)
                    copy_v(n, 0, 1)
                if live(m):
                    take_p(m, 2)
                if live(n):
                    square(n, 1, 2)
                    split_hi(nx, (0, 1))
                    take_qk(n, 0, 2)
                if live(m - 1):
                    affine(m - 1)
                if live(n):
                    square(n, 1, 3)
                if live(m):
                    take_o(m, 2)
                if live(n):
                    take_qk(n, 0, 3)
                    copy_v(n, 1, 0)
                if live(nx):
                    shifted(nx, 0)
                    shifted(nx, 1)
                if live(n):
                    copy_v(n, 1, 1)
                if live(m - 1):
                    gelu(m - 1)
                if live(m):
                    take_p(m, 3)
                if live(nx):
                    split_hi(nx, (2, 3))
                    square(nx, 0, 0)
                    split_hi(nx, (4, 5))
                    square(nx, 0, 1)
                if live(n):
                    exps(n, 0)
                    take_qk(n, 1, 0)
                if live(m):
                    take_o(m, 3)
                if live(m - 1):
                    take_h(m - 1)
                if live(n):
                    take_qk(n, 1, 1)
                    take_qk(n, 1, 2)
                    exps(n, 1)
                if live(nx):
                    square(nx, 0, 2)
                if live(n):
                    take_qk(n, 1, 3)
                if live(nx):
                    square(nx, 0, 3)
                if live(n):
                    take_p(n, 0)
                if live(m):
                    shifted_f(m)
                if live(nx + 1):
                    copy_in(nx + 1)
                if live(nx):
                    square(nx, 1, 0)
                    take_qk(nx, 0, 0)
                if live(n):
                    take_p(n, 1)
                    exps(n, 2)
                    take_o(n, 0)
                if live(m):
                    residual(m)
                if live(nx):
                    copy_v(nx, 0, 0)

            split_hi(0, (0, 1))
            for n in range(-2, FIRST):
                iteration(n)
            with act.Fori(FIRST, LAST) as n:
                iteration(n)
            for n in range(LAST, STEPS + 2):
                iteration(n)

        @block.vector
        def _(dve):
            d = nc.vector
            d.memset(vb[:, :], 0.0)
            d.memset(pz[:, :], 0.0)
            dve.wait_ge(s_x, 16)
            for k in range(SEQS * TILES):
                d.bn_stats(st0[:, k * 6:(k + 1) * 6], acc[:, k * P:(k + 1) * P]).then_inc(s_l0, 1)
            dve.wait_ge(s_l0, SEQS * TILES)
            for k in range(SEQS * TILES):
                d.bn_aggr(mv0[:, k * 2:(k + 1) * 2], st0[:, k * 6:(k + 1) * 6]).then_inc(s_l0, 1)

            d.memset(ht[:, :], 1.0)
            dve.wait_ge(s_const, 16 * NCONST)
            d.tensor_copy(identh[:, :], ident[:, :])
            d.tensor_scalar(x_hi[:, 0:1], ident[:, 0:1], 0.0, None, ALU.mult)
            d.tensor_scalar(x_lo[:, 0:1], ident[:, 0:1], 0.0, None, ALU.mult)
            d.tensor_copy(mask[:, :], maskf[:, :]).then_inc(s_zero, 1)

            def first_normalise(s):
                for k in range(TILES * s, TILES * (s + 1)):
                    last = d.tensor_scalar(x_tok[:, k * P:(k + 1) * P], acc[:, k * P:(k + 1) * P],
                                           mv0[:, 2 * k:2 * k + 1], rs0[:, k:k + 1], ALU.subtract, ALU.mult)
                last.then_inc(s_xready, 1)

            def first_take_in(s):
                dve.wait_ge(s_xready, nth(1, s, 1))
                dve.wait_ge(s_a["t"], nth(1, s - 1, 1))
                d.tensor_copy(axin[:, :], x_tok[:, bass.ds(s * LEN, LEN)]).then_inc(s_a["xin"], 1)

            def first_maxima(s):
                dve.wait_ge(s_a["s"], nth(1, s, 1))
                dve.wait_ge(s_a["exp"], nth(2, s - 1, 2))
                d.tensor_reduce(am2[:, :], pS[:, :].rearrange("p (t k) -> p t k", t=TILES), op=ALU.max, axis=AX.X)\
                 .then_inc(s_a["max"], 1)
                dve.wait_ge(s_a["max"], nth(1, s, 1))
                d.tensor_scalar(am2[:, :], am2[:, :], -float(P) ** -0.5, None, ALU.mult).then_inc(s_a["neg"], 1)

            def first_bias(s):
                dve.wait_ge(s_a["qkv"], nth(3, s, 3))
                dve.wait_ge(s_a["o"], nth(1, s - 2, 1))
                d.tensor_tensor(av[:, bass.ds((s % 2) * LEN, LEN)].rearrange("p (t c) -> p t c", t=TILES),
                                pG[:, 0:LEN].rearrange("p (t c) -> p t c", t=TILES),
                                abv[:, :].unsqueeze(1).to_broadcast([P, TILES, P]), ALU.add).then_inc(s_a["v"], 1)

            def first_add(s):
                dve.wait_ge(s_a["rec"], nth(1, s, 1))
                dve.wait_ge(s_a["o"], nth(1, s, 1))
                for T in range(TILES):
                    o = acc[:, bass.ds(s * LEN + T * P, P)]
                    last = d.scalar_tensor_tensor(out=o, in0=pO[:, T * P:(T + 1) * P], scalar=ar2[:, T:T + 1],
                                                  in1=o, op0=ALU.mult, op1=ALU.add)
                last.then_inc(s_a["done"], 1)

            def first_reciprocals(s):
                dve.wait_ge(s_a["exp"], nth(2, s, 2))
                dve.wait_ge(s_a["done"], nth(1, s - 1, 1))
                d.reciprocal(ar2[:, :], as2[:, :]).then_inc(s_a["rec"], 1)

            def first_attention(s):
                if some(s):
                    first_maxima(s)
                if some(s + 2):
                    first_take_in(s + 2)
                if some(s + 1):
                    first_bias(s + 1)
                if some(s - 1):
                    first_add(s - 1)
                if some(s):
                    first_reciprocals(s)

            dve.wait_ge(s_l0p, 2)
            first_normalise(0)
            first_attention(-2)
            for s in range(1, SEQS):
                first_normalise(s)
            for s in (-1, 0, 1):
                first_attention(s)
            with dve.Fori(2, SEQS - 2) as s:
                first_attention(s)
            for s in (SEQS - 2, SEQS - 1, SEQS):
                first_attention(s)
            dve.wait_ge(s_rbase, 1)

            def split_lo(n, chunks):
                def body():
                    for c in chunks:
                        dve.wait_ge(s_zero, 2)
                        dve.wait_ge(s_wh, layer(n) * WCH + c + 1)
                        w = slice(c * CH, (c + 1) * CH)
                        d.tensor_tensor(w_lo[:, w], w_new[:, w], w_hi[:, w].bitcast(F32), ALU.subtract)\
                         .then_inc(s_wl, 1)

                if not isinstance(n, int):
                    with dve.If(n % SEQS == 0):
                        body()
                elif n % SEQS == 0 and live(n):
                    body()

            def rest(n):
                dve.wait_ge(s_xs, nth(4, n, 4))
                d.tensor_tensor(x_lo[0:64, :], pT[0:64, 0:LEN], x_hi[0:64, :].bitcast(F32), ALU.subtract)\
                 .then_inc(s_xl, 1)
                d.tensor_tensor(x_lo[64:P, 1:LEN], pT[64:P, 0:LEN - 1], x_hi[64:P, 1:LEN].bitcast(F32),
                                ALU.subtract).then_inc(s_xl, 1)

            def rotate(n, T, m):
                i, kind, b = 4 * T + m, 2 * (m // 2), (m % 2) * CH
                dve.wait_ge(s_sq, nth(8, n, i + 1))
                dve.wait_ge(s_add, nth(8, n, i - 1))
                src = heads(pQ[m % 2][:, :])
                d.tensor_tensor(heads(t1[:, b:b + CH]), src, table(n, kind, T), ALU.mult).then_inc(s_t1, 1)
                o2 = heads(t2[:, b:b + CH])
                d.tensor_tensor(o2[:, :, 0:HD], src[:, :, HD:], table(n, kind + 1, T, 0), ALU.mult)
                d.tensor_tensor(o2[:, :, HD:], src[:, :, 0:HD], table(n, kind + 1, T, 1), ALU.mult)\
                 .then_inc(s_rot, 1)
                d.tensor_reduce(n2[:, T * 2 * HEADS + m * CHH:T * 2 * HEADS + (m + 1) * CHH],
                                heads(sq[:, b:b + CH]), op=ALU.add, axis=AX.X).then_inc(s_n2, 1)

            def guard(n, T, k):
                c = 2 * T + k
                w = slice(c * HEADS, (c + 1) * HEADS)
                dve.wait_ge(s_n2, nth(8, n, 2 * c + 2))
                dve.wait_ge(s_rn, nth(4, n - 1, c + 1))
                d.tensor_scalar(n2c[:, w], n2[:, w], 1e-24, None, ALU.max).then_inc(s_n2c, 1)

            def scale_k(n, T, m):
                dve.wait_ge(s_add, nth(8, n, 4 * T + m + 1))
                dve.wait_ge(s_rn, nth(4, n, 2 * T + 2))
                c = heads(rot[:, (4 * T + m) * CH:(4 * T + m + 1) * CH])
                r = rnorm[:, T * 2 * HEADS + m * CHH:T * 2 * HEADS + (m + 1) * CHH]
                d.tensor_tensor(c, c, over(r, CHH, DH), ALU.mult).then_inc(s_ksc, 1)

            def eight(t, u):
                return t[:, (u % 2) * PAIRS:(u % 2 + 1) * PAIRS]

            def maxima(n, u):
                dve.wait_ge(s_s, nth(4, n, u + 1))
                d.tensor_reduce(eight(m8, u), heads(pS[:, :]), op=ALU.max, axis=AX.X).then_inc(s_max, 1)

            def less_max(n, u):
                dve.wait_ge(s_max, nth(4, n, u + 1))
                dve.wait_ge(s_pt, nth(4, n, u - 1))
                d.tensor_tensor(heads(es[:, (u % 2) * CH:(u % 2 + 1) * CH]), heads(pS[:, :]),
                                over(eight(m8, u), PAIRS, DH), ALU.subtract).then_inc(s_sub, 1)

            def sums(n, u):
                dve.wait_ge(s_exp, nth(4, n, u + 1))
                d.tensor_reduce(eight(s8, u), heads(es[:, (u % 2) * CH:(u % 2 + 1) * CH]), op=ALU.add, axis=AX.X)\
                 .then_inc(s_sum, 1)

            def reciprocals(n, u):
                dve.wait_ge(s_sum, nth(4, n, u + 1))
                d.reciprocal(eight(r8, u), eight(s8, u)).then_inc(s_rec, 1)

            def middle(n, T):
                dve.wait_ge(s_wo, nth(2, n, T + 1))
                dve.wait_ge(s_f1, nth(1, n - 1, 1))
                dve.wait_ge(s_res, nth(1, n - 1, 1))
                d.tensor_tensor(xm[:, T * P:(T + 1) * P], pO[:, 0:P], tokens(x_tok, n, T), ALU.add)\
                 .then_inc(s_mid, 1)

            def stats(n):
                dve.wait_ge(s_f2, nth(1, n, 1))
                for T in range(TILES):
                    d.bn_stats(stat[:, T * 6:(T + 1) * 6], pF[:, T * P:(T + 1) * P]).then_inc(s_st, 1)

            def moments(n):
                dve.wait_ge(s_zero, 2)
                dve.wait_ge(s_st, nth(2, n, 2))
                for T in range(TILES):
                    d.bn_aggr(mv[:, T * 2:(T + 1) * 2], stat[:, T * 6:(T + 1) * 6]).then_inc(s_mv, 1)

            def normalise(n):
                dve.wait_ge(s_rstd, nth(1, n, 1))
                for T in range(TILES):
                    d.tensor_scalar(xn[:, T * P:(T + 1) * P], pF[:, T * P:(T + 1) * P], mv[:, 2 * T:2 * T + 1],
                                    rstd[:, T:T + 1], ALU.subtract, ALU.mult).then_inc(s_xn, 1)

            def bias_gate(n):
                dve.wait_ge(s_f4g, nth(1, n, 1))
                for T in range(TILES):
                    d.tensor_tensor(gt[:, T * HID:(T + 1) * HID], pH[T][:, 0:HID],
                                    b_1[:, bass.ds(par(n) * 2 * HID + HID, HID)], ALU.add).then_inc(s_gt, 1)

            def bias_hidden(n):
                dve.wait_ge(s_f4a, nth(1, n, 1))
                for T in range(TILES):
                    d.tensor_tensor(am[:, T * HID:(T + 1) * HID], pH[T][:, 0:HID],
                                    b_1[:, bass.ds(par(n) * 2 * HID, HID)], ALU.add).then_inc(s_am, 1)

            def gated(n):
                dve.wait_ge(s_gg, nth(1, n, 1))
                dve.wait_ge(s_am, nth(2, n, 2))
                d.tensor_tensor(am[:, :], am[:, :], gt[:, :], ALU.mult).then_inc(s_hm, 1)

            def finish(n):
                dve.wait_ge(s_f6, nth(1, n, 1))
                dve.wait_ge(s_res, nth(1, n, 1))
                for T in range(TILES):
                    o = tokens(x_tok, n, T)
                    last = d.tensor_tensor(o, pH[T][:, 0:P], o, ALU.add)
                last.then_inc(s_xready, 1)

            def iteration(n):
                nx, m = n + 1, n - 1
                if live(n):
                    scale_k(n, 0, 2)
                if live(m):
                    less_max(m, 3)
                if live(n):
                    rotate(n, 1, 1)
                if live(m - 1):
                    normalise(m - 1)
                if live(n):
                    guard(n, 1, 0)
                    scale_k(n, 0, 3)
                if live(m):
                    sums(m, 3)
                    middle(m, 0)
                    reciprocals(m, 3)
                if live(n):
                    rotate(n, 1, 2)
                    split_lo(nx, (0, 1))
                    rotate(n, 1, 3)
                if live(m - 1):
                    bias_gate(m - 1)
                if live(nx):
                    rest(nx)
                if live(n):
                    guard(n, 1, 1)
                    maxima(n, 0)
                if live(m - 1):
                    bias_hidden(m - 1)
                if live(n):
                    less_max(n, 0)
                if live(m - 1):
                    gated(m - 1)
                if live(nx):
                    split_lo(nx, (2, 3))
                    rotate(nx, 0, 0)
                    split_lo(nx, (4, 5))
                    rotate(nx, 0, 1)
                if live(n):
                    maxima(n, 1)
                if live(nx):
                    guard(nx, 0, 0)
                if live(n):
                    less_max(n, 1)
                    scale_k(n, 1, 2)
                    sums(n, 0)
                    reciprocals(n, 0)
                    scale_k(n, 1, 3)
                if live(m - 1):
                    finish(m - 1)
                if live(n):
                    sums(n, 1)
                if live(m):
                    middle(m, 1)
                if live(nx):
                    rotate(nx, 0, 2)
                if live(n):
                    reciprocals(n, 1)
                if live(nx):
                    rotate(nx, 0, 3)
                if live(n):
                    maxima(n, 2)
                if live(nx):
                    guard(nx, 0, 1)
                if live(n):
                    less_max(n, 2)
                if live(nx):
                    rotate(nx, 1, 0)
                if live(m):
                    stats(m)
                if live(n):
                    sums(n, 2)
                    reciprocals(n, 2)
                if live(m):
                    moments(m)
                if live(n):
                    maxima(n, 3)

            split_lo(0, (0, 1))
            for n in range(-2, FIRST):
                iteration(n)
            with dve.Fori(FIRST, LAST) as n:
                iteration(n)
            for n in range(LAST, STEPS + 2):
                iteration(n)
            dve.wait_ge(s_xready, STEPS + SEQS)
            d.tensor_tensor(acc[:, :], acc[:, :], x_tok[:, :], ALU.add).then_inc(s_fin, 1)

        @block.tensor
        def _(pe):
            t = nc.tensor

            def mm(o, l, r, start=True, stop=True):
                return t.matmul(o, l, r, start=start, stop=stop, skip_group_check=True)

            pe.wait_ge(s_const, 16 * NCONST)
            pe.wait_ge(s_zero, 2)

            def first_turn_p(s):
                pe.wait_ge(s_a["exp"], nth(2, s, 2))
                pe.wait_ge(s_a["pte"], nth(1, s - 1, 1))
                for k in range(TILES):
                    for T in range(TILES):
                        last = t.transpose(pP[:, (k * TILES + T) * P:(k * TILES + T + 1) * P],
                                           aprob[:, T * LEN + k * P:T * LEN + (k + 1) * P], ident[:, :])
                last.then_inc(s_a["pt"], 1)

            def first_turn_x(s):
                pe.wait_ge(s_a["xin"], nth(1, s, 1))
                pe.wait_ge(s_a["x"], nth(1, s - 1, 1))
                for T in range(TILES):
                    last = t.transpose(pT[:, T * P:(T + 1) * P], axin[:, T * P:(T + 1) * P], ident[:, :])
                last.then_inc(s_a["t"], 1)

            def first_scores(s):
                pe.wait_ge(s_a["q"], nth(1, s, 1))
                pe.wait_ge(s_a["k"], nth(1, s, 1))
                pe.wait_ge(s_a["exp"], nth(2, s - 1, 2))
                for T in range(TILES):
                    last = mm(pS[:, T * LEN:(T + 1) * LEN], aq[:, T * P:(T + 1) * P], ak[:, :])
                last.then_inc(s_a["s"], 1)

            def first_values(s):
                pe.wait_ge(s_a["pte"], nth(1, s, 1))
                pe.wait_ge(s_a["v"], nth(1, s, 1))
                pe.wait_ge(s_a["done"], nth(1, s - 1, 1))
                for T in range(TILES):
                    for k in range(TILES):
                        last = mm(pO[:, T * P:(T + 1) * P], apt[:, (k * TILES + T) * P:(k * TILES + T + 1) * P],
                                  av[:, bass.ds((s % 2) * LEN + k * P, P)], start=k == 0, stop=k == TILES - 1)
                last.then_inc(s_a["o"], 1)

            def first_project(s):
                pe.wait_ge(s_a["x"], nth(1, s, 1))
                pe.wait_ge(s_a["q"], nth(1, s - 1, 1))
                pe.wait_ge(s_a["k"], nth(1, s - 1, 1))
                pe.wait_ge(s_a["v"], nth(1, s - 1, 1))
                mm(pQ[0][:, 0:LEN], aw[:, 0:P], ax[:, :]).then_inc(s_a["qkv"], 1)
                mm(pQ[1][:, 0:LEN], aw[:, P:2 * P], ax[:, :]).then_inc(s_a["qkv"], 1)
                for T in range(TILES):
                    last = mm(pG[:, T * P:(T + 1) * P], ax[:, T * P:(T + 1) * P], aw[:, 2 * P:3 * P])
                last.then_inc(s_a["qkv"], 1)

            def first_attention(s):
                if some(s - 1):
                    first_turn_p(s - 1)
                if some(s + 1):
                    first_turn_x(s + 1)
                if some(s):
                    first_scores(s)
                if some(s + 1):
                    first_project(s + 1)
                if some(s - 1):
                    first_values(s - 1)

            for s in (-1, 0, 1):
                first_attention(s)
            with pe.Fori(2, SEQS - 1) as s:
                first_attention(s)
            for s in (SEQS - 1, SEQS):
                first_attention(s)
            pe.wait_ge(s_a["done"], SEQS)
            pe.wait_ge(s_w, 2 * 16 * WLOADS)

            def take_in(n):
                pe.wait_ge(s_xin, nth(1, n, 1))
                pe.wait_ge(s_qte, nth(12, n - 1, 6))
                for T in range(TILES):
                    last = t.transpose(pT[:, T * P:(T + 1) * P], xin[:, T * P:(T + 1) * P], ident[:, :])
                last.then_inc(s_xt, 1)

            def product(o, T, c):
                x, w = slice(T * P, (T + 1) * P), slice(c * CH, (c + 1) * CH)
                mm(o[:, :], x_hi[:, x], w_hi[:, w], stop=False)
                mm(o[:, :], x_hi[:, x], w_lo[:, w], start=False, stop=False)
                return mm(o[:, :], x_lo[:, x], w_hi[:, w], start=False)

            def project(n, T, i):
                pe.wait_ge(s_xl, nth(2, n, 2))
                if T == 0:
                    pe.wait_ge(s_wl, layer(n) * WCH + i + 1)
                pe.wait_ge(s_rot, nth(8, n, 4 * T + i - 1))
                product(pQ[i % 2], T, i).then_inc(s_qk, 1)

            def project_v(n, T, c):
                pe.wait_ge(s_xl, nth(2, n, 2))
                if T == 0:
                    pe.wait_ge(s_wl, layer(n) * WCH + 4 + c + 1)
                if T == 0 and c == 0:
                    pe.wait_ge(s_xready, nth(1, n - 3, SEQS + 1))
                elif T == 0:
                    pe.wait_ge(s_v, nth(4, n, 1))
                elif c == 0:
                    pe.wait_ge(s_sub, nth(4, n - 1, 4))
                else:
                    pe.wait_ge(s_ot, nth(4, n - 1, 3))
                product(pV[2 * T + c], T, 4 + c).then_inc(s_vp, 1)

            def turn_qk(n, T, g):
                if g < 2:
                    pe.wait_ge(s_qsc, nth(4, n, 2 * T + g + 1))
                else:
                    pe.wait_ge(s_ksc, nth(4, n, 2 * T + g - 1))
                if g == 0 and T == 0:
                    pe.wait_ge(s_qte, nth(12, n - 1, 12))
                elif g == 0:
                    pe.wait_ge(s_qte, nth(12, n, 6))
                    if live(n + 1):
                        pe.wait_ge(s_xl, nth(2, n + 1, 2))
                else:
                    pe.wait_ge(s_qte, nth(12, n, 6 * T + (2 * g if g < 3 else 5)))
                for k in range(4):
                    last = t.transpose(pT[:, k * P:(k + 1) * P],
                                       rot[:, (4 * T + g) * CH + k * P:(4 * T + g) * CH + (k + 1) * P], ident[:, :])
                last.then_inc(s_qt, 1)

            def scores(n, u):
                T, al = u // 2, 1 - u % 2
                pe.wait_ge(s_qte, nth(12, n, 6 * T + 6))
                if u == 0:
                    pe.wait_ge(s_v, nth(4, n, 3))
                else:
                    pe.wait_ge(s_sub, nth(4, n, u))
                first = int(T == 0 and al == 0)
                mm(pS[:, :], identh[:, :],
                   mask[:, first * 64:first * 64 + 64].unsqueeze(1).to_broadcast([P, PAIRS, 64]),
                   stop=False)
                for pair in range(PAIRS):
                    for s in range(2):
                        w = 4 * T + al + 2 * s
                        last = mm(pS[64 * s:64 * s + 64, pair * 64:pair * 64 + 64],
                                  qz[:, (pair * 8 + w) * 64:(pair * 8 + w) * 64 + 64],
                                  kt3[:, pair, WIN * w:WIN * w + 64], start=False, stop=pair == PAIRS - 1)
                last.then_inc(s_s, 1)

            def turn_p(n, u):
                pe.wait_ge(s_p, nth(4, n, u + 1))
                pe.wait_ge(s_pte, nth(16, n, 4 * u))
                for k in range(4):
                    c = (u % 2) * CH + k * P
                    last = t.transpose(pP[:, k * P:(k + 1) * P], es[:, c:c + P], ident[:, :])
                last.then_inc(s_pt, 1)

            def values(n, u):
                T, al = u // 2, 1 - u % 2
                pe.wait_ge(s_pte, nth(16, n, 4 * u + 4))
                if al:
                    pe.wait_ge(s_v, nth(4, n, 2 * T + 2))
                elif T:
                    pe.wait_ge(s_vb1, nth(32, n, 32))
                else:
                    pe.wait_ge(s_vb0, nth(16, n, 16))
                if u < 3:
                    pe.wait_ge(s_ot, nth(4, n, u))
                elif live(n + 1):
                    pe.wait_ge(s_v, nth(4, n + 1, 4))
                else:
                    pe.wait_ge(s_ot, nth(4, n, 3))
                if al:
                    pe.wait_ge(s_mid, nth(2, n, T))
                src = v if al else vb
                for h in range(HEADS):
                    pair, hh = h // 2, h % 2
                    last = mm(pO[64 * hh:64 * hh + 64, pair * 64:pair * 64 + 64],
                              src[:, T * INNER + h * DH:T * INNER + (h + 1) * DH],
                              pz5[:, u % 2, pair, :, hh, :])
                last.then_inc(s_av, 1)

            def project_out(n, T):
                if T == 0:
                    pe.wait_ge(s_w, layer(n) * (16 * WLOADS) + 16 * WLOADS)
                pe.wait_ge(s_ot, nth(4, n, 2 * T + 2))
                for pair in range(PAIRS):
                    last = mm(pO[:, 0:P], ot[:, pair * LEN + T * P:pair * LEN + (T + 1) * P],
                              w_o[:, bass.ds(par(n) * (PAIRS * P) + pair * P, P)],
                              start=pair == 0, stop=pair == PAIRS - 1)
                last.then_inc(s_wo, 1)

            def turn_to_pF(src, signal):
                for T in range(TILES):
                    last = t.transpose(pF[:, T * P:(T + 1) * P], src[:, T * P:(T + 1) * P], ident[:, :])
                last.then_inc(signal, 1)

            def turn_mid(n):
                pe.wait_ge(s_mid, nth(2, n, 2))
                pe.wait_ge(s_xready, nth(1, n - 1, SEQS + 1))
                turn_to_pF(xm, s_f1)

            def turn_shifted(n):
                pe.wait_ge(s_xf, nth(2, n, 2))
                turn_to_pF(xf, s_f2)

            def turn_normal(n):
                pe.wait_ge(s_xn, nth(2, n, 2))
                turn_to_pF(xn, s_f3)

            def hidden(n, half):
                if half:
                    pe.wait_ge(s_xg, nth(1, n, 1))
                    if live(n + 2):
                        pe.wait_ge(s_v, nth(4, n + 2, 2))
                else:
                    pe.wait_ge(s_gt, nth(2, n, 2))
                for T in range(TILES):
                    last = mm(pH[T][:, 0:HID], xg[:, T * P:(T + 1) * P],
                              w_1[:, bass.ds(par(n) * 2 * HID + half * HID, HID)])
                last.then_inc(s_f4g if half else s_f4a, 1)

            def turn_h(n):
                pe.wait_ge(s_hm, nth(1, n, 1))
                for T in range(TILES):
                    for j in range(HCH):
                        w = P if j < 2 else HLAST
                        c = T * HID + j * P
                        last = t.transpose(pH[T][0:w, j * P:(j + 1) * P], am[:, c:c + w], ident[:, :])
                last.then_inc(s_f5, 1)

            def down(n):
                pe.wait_ge(s_ht, nth(4, n, 4))
                for T in range(TILES):
                    for j in range(HCH):
                        k = P if j < 2 else HLAST + 1
                        c = (T * HCH + j) * P
                        last = mm(pH[T][:, 0:P], ht[0:k, c:c + P],
                                  w_2[0:k, bass.ds(par(n) * (HCH * P) + j * P, P)], start=j == 0, stop=j == HCH - 1)
                last.then_inc(s_f6, 1)

            def iteration(n):
                nx, m = n + 1, n - 1
                if live(n):
                    turn_qk(n, 0, 1)
                if live(m):
                    project_out(m, 0)
                    turn_p(m, 2)
                if live(n):
                    project_v(n, 1, 0)
                    turn_qk(n, 0, 2)
                if live(m - 1):
                    turn_normal(m - 1)
                if live(n):
                    project(n, 1, 3)
                if live(m):
                    values(m, 2)
                if live(n):
                    turn_qk(n, 0, 3)
                if live(m - 1):
                    hidden(m - 1, 1)
                if live(n):
                    project_v(n, 1, 1)
                if live(nx):
                    take_in(nx)
                if live(n):
                    scores(n, 0)
                if live(m - 1):
                    hidden(m - 1, 0)
                if live(m):
                    turn_p(m, 3)
                if live(nx):
                    project(nx, 0, 0)
                if live(n):
                    turn_qk(n, 1, 0)
                if live(nx):
                    project(nx, 0, 1)
                if live(m):
                    values(m, 3)
                if live(n):
                    scores(n, 1)
                if live(m - 1):
                    turn_h(m - 1)
                if live(nx):
                    project(nx, 0, 2)
                if live(n):
                    turn_qk(n, 1, 1)
                if live(nx):
                    project(nx, 0, 3)
                if live(m - 1):
                    down(m - 1)
                if live(n):
                    turn_qk(n, 1, 2)
                if live(m):
                    project_out(m, 1)
                if live(n):
                    turn_qk(n, 1, 3)
                if live(nx):
                    project_v(nx, 0, 0)
                if live(m):
                    turn_mid(m)
                if live(n):
                    turn_p(n, 0)
                if live(nx):
                    turn_qk(nx, 0, 0)
                    project(nx, 1, 0)
                if live(n):
                    scores(n, 2)
                    turn_p(n, 1)
                if live(m):
                    turn_shifted(m)
                if live(nx):
                    project(nx, 1, 1)
                if live(n):
                    values(n, 0)
                    scores(n, 3)
                    values(n, 1)
                if live(nx):
                    project(nx, 1, 2)
                    project_v(nx, 0, 1)

            for n in range(-2, FIRST):
                iteration(n)
            with pe.Fori(FIRST, LAST) as n:
                iteration(n)
            for n in range(LAST, STEPS + 2):
                iteration(n)


def constants():
    f = np.float32
    half = np.arange(0, DH, 2, dtype=f)
    inv_freq = (f(1.0) / np.power(f(10000.0), half / f(DH))).astype(f)
    t = np.arange(LEN, dtype=f)
    freqs = (t[:, None] * inv_freq[None, :]).astype(f)
    base = ((half + f(0.4 * DH)) / f(1.4 * DH)).astype(f)
    power = (t - f(LEN // 2)) / f(WIN // 2)
    scale = np.power(base[None, :], power[:, None]).astype(f)
    cos, sin = np.cos(freqs), np.sin(freqs)
    rows = []
    for s in (scale, f(1.0) / scale):
        rows.append(np.concatenate([cos * s, cos * s], 1))
        rows.append(np.concatenate([-sin * s, sin * s], 1))
    rot_base = np.stack(rows).reshape(4, TILES, P, DH).transpose(2, 0, 1, 3).reshape(P, -1).astype(f)
    q = np.arange(P) % WIN
    j = np.arange(2 * WIN)
    seen = np.where(j[None, :] < WIN, q[:, None] <= j[None, :], j[None, :] - WIN <= q[:, None])
    first = seen & ((np.arange(P)[:, None] >= 64) | (j[None, :] >= WIN))
    masks = np.where(np.concatenate([seen, first], 1), 0.0, MASKED).astype(f)
    return {"rot_base": rot_base, "masks": masks, "ident_f": np.eye(P, dtype=f)}


_INS = ["X", "W_q", "W_k", "W_v", "b_q", "b_k", "b_v"]
_FFN = ["Wqkv", "q_scale", "k_scale", "Wo", "ln_g", "ln_b", "W1", "b1", "W2", "b2"]
_FLAT = {"Wqkv": (DEPTH * P, QKV), "Wo": (DEPTH * INNER, P), "W1": (DEPTH * P, 2 * HID), "W2": (DEPTH * HID, P)}


def kernel(**inputs):
    import concourse.bacc as _bacc
    from concourse.bass_utils import run_bass_kernel_spmd as _run

    nc = _bacc.Bacc("TRN2", target_bir_lowering=False, num_devices=1)
    arrays = {}
    for n in _INS:
        arrays[n] = np.ascontiguousarray(inputs["L0_attn_" + n])
    for n in _FFN:
        a = np.ascontiguousarray(inputs["L0_ffn_" + n])
        arrays[n] = a.reshape(_FLAT[n]) if n in _FLAT else a
    arrays.update(constants())
    arrays = {f"in_{n}": a for n, a in arrays.items()}
    args = [nc.dram_tensor(n, a.shape, mybir.dt.from_np(a.dtype), kind="ExternalInput").ap()
            for n, a in arrays.items()]
    out = nc.dram_tensor("out", (SEQS, LEN, P), F32, kind="ExternalOutput").ap()
    program(nc, *args, out)
    r = _run(nc, [arrays], core_ids=[0])
    return r.results[0]["out"]
```
